# Optimizing a Trainium2 kernel written in Bass

```python
import numpy as np
import jax
import jax.numpy as jnp

def _softmax(x, axis=-1):
    return jax.nn.softmax(x, axis=axis)

def _gelu(x):
    return jax.nn.gelu(x, approximate=True)

def _silu(x):
    return jax.nn.silu(x)

def _sigmoid(x):
    return jax.nn.sigmoid(x)

def _layernorm(x, axis=-1, eps=1e-05):
    m = jnp.mean(x, axis=axis, keepdims=True)
    v = jnp.var(x, axis=axis, keepdims=True)
    return (x - m) / jnp.sqrt(v + eps)

def _scatter_add(tgt, idx, src, axis=0):
    return tgt.at[idx].add(src)

def _segment_sum(src, seg, n):
    return jax.ops.segment_sum(src, seg, n)
kernel_name = 'mk_xattn_ffn_d1_seqx_r8_5ac541'

def setup_inputs(seed: int=0):
    np.random.seed(seed)
    _w = jnp.asarray

    def _rec_inputs():
        import jax
        import jax.numpy as jnp
        _rk = jax.random.key(seed)
        x = -0.0005207 + 1.001 * jax.random.normal(jax.random.fold_in(_rk, 1), (8, 56, 256), jnp.float32)
        _lenS = 56 - jax.random.randint(jax.random.fold_in(_rk, 7), (8,), 0, max(1, 56 // 4) + 1, jnp.int32)
        _lenS2 = 1500 - jax.random.randint(jax.random.fold_in(_rk, 8), (8,), 0, max(1, 1500 // 4) + 1, jnp.int32)
        _ctx_2048P = jax.random.normal(jax.random.fold_in(_rk, 12), (8, 16, 256), jnp.float32)
        _ctx_2048c = jax.random.dirichlet(jax.random.fold_in(_rk, 512), 0.3 * jnp.ones((16,), jnp.float32), (8, 1500))
        _ctx_2048t = jnp.einsum('bsk,bkd->bsd', _ctx_2048c, _ctx_2048P)
        _ctx_2048t = _ctx_2048t * jax.lax.rsqrt(jnp.mean(jnp.square(_ctx_2048t)) + 1e-12) * 0.953939
        ctx_2048 = -5.72187e-05 + 0.999849 * (_ctx_2048t + 0.3 * jax.random.normal(jax.random.fold_in(_rk, 612), (8, 1500, 256), jnp.float32))
        _validS = jnp.arange(56)[None, :] < _lenS[:, None]
        _validS2 = jnp.arange(1500)[None, :] < _lenS2[:, None]
        _causal = jnp.tril(jnp.ones((56, 56), dtype=bool))
        mask_BxSx4224_bf0 = jnp.logical_not(jnp.ones((8, 56, 528), dtype=bool))
        return (x, ctx_2048, mask_BxSx4224_bf0)
    x, ctx_2048, mask_BxSx4224_bf0 = _rec_inputs()

    def _L0_xattn_setup():
        import jax, jax.numpy as jnp
        import numpy as np
        import math
        DIM = 256
        B, Q_LEN, KV_LEN = (8, 128, 512)
        key = jax.random.key(seed)
        ks = jax.random.split(key, 8)
        x = jax.random.normal(ks[0], (B, Q_LEN, DIM), dtype=jnp.float32)
        mask = jnp.zeros((B, Q_LEN, KV_LEN + Q_LEN), dtype=bool)
        k_cache = jax.random.normal(ks[1], (B, KV_LEN, DIM), dtype=jnp.float32)
        v_cache = jax.random.normal(ks[2], (B, KV_LEN, DIM), dtype=jnp.float32)
        scale = 1.0 / math.sqrt(DIM)
        wq = jax.random.normal(ks[3], (DIM, DIM), dtype=jnp.float32) * scale
        wk = jax.random.normal(ks[4], (DIM, DIM), dtype=jnp.float32) * scale
        wv = jax.random.normal(ks[5], (DIM, DIM), dtype=jnp.float32) * scale
        wo = jax.random.normal(ks[6], (DIM, DIM), dtype=jnp.float32) * scale
        return {'x': x, 'mask': mask, 'k_cache': k_cache, 'v_cache': v_cache, 'wq': wq, 'wk': wk, 'wv': wv, 'wo': wo}
    _L0_xattn_all = _L0_xattn_setup()
    _L0_xattn_in = {k: v for k, v in _L0_xattn_all.items() if k in ('wq', 'wk', 'wv', 'wo')}
    del _L0_xattn_all

    def _L0_ffn_setup():
        import jax, jax.numpy as jnp
        import numpy as np
        TOP_P = 0.9
        S, B, H, I, E = (256, 4, 256, 512, 8)

        def _top_p_weights(probs, top_p):
            order = jnp.argsort(-probs, axis=-1)
            sp = jnp.take_along_axis(probs, order, axis=-1)
            cum = jnp.cumsum(sp, axis=-1)
            exceed = cum > top_p
            first_idx = jnp.argmax(exceed, axis=-1)
            first = jnp.arange(probs.shape[-1])[None, :] == first_idx[:, None]
            keep = ~exceed | first
            kept = jnp.where(keep, sp, 0.0)
            t_idx = jnp.arange(probs.shape[0])[:, None]
            return jnp.zeros_like(probs).at[t_idx, order].set(kept)
        key = jax.random.key(seed)
        ks = jax.random.split(key, 5)
        scale = 0.02
        return {'hidden_states': jax.random.normal(ks[0], (S, B, H), dtype=jnp.float32), 'router_w': jax.random.normal(ks[1], (E, H), dtype=jnp.float32) * scale, 'gate_w': jax.random.normal(ks[2], (E, I, H), dtype=jnp.float32) * scale, 'up_w': jax.random.normal(ks[3], (E, I, H), dtype=jnp.float32) * scale, 'down_w': jax.random.normal(ks[4], (E, H, I), dtype=jnp.float32) * scale}
    _L0_ffn_all = _L0_ffn_setup()
    _L0_ffn_in = {k: v for k, v in _L0_ffn_all.items() if k in ('router_w', 'gate_w', 'up_w', 'down_w')}
    del _L0_ffn_all
    return {'x': x, 'ctx_2048': ctx_2048, 'mask_BxSx4224_bf0': mask_BxSx4224_bf0, 'L0_xattn_wq': _L0_xattn_in['wq'], 'L0_xattn_wk': _L0_xattn_in['wk'], 'L0_xattn_wv': _L0_xattn_in['wv'], 'L0_xattn_wo': _L0_xattn_in['wo'], 'L0_ffn_router_w': _L0_ffn_in['router_w'], 'L0_ffn_gate_w': _L0_ffn_in['gate_w'], 'L0_ffn_up_w': _L0_ffn_in['up_w'], 'L0_ffn_down_w': _L0_ffn_in['down_w']}

def reference(x, ctx_2048, mask_BxSx4224_bf0, L0_xattn_wq, L0_xattn_wk, L0_xattn_wv, L0_xattn_wo, L0_ffn_router_w, L0_ffn_gate_w, L0_ffn_up_w, L0_ffn_down_w):
    import jax
    import jax.numpy as jnp

    def _L0_xattn_ref(x, mask, k_cache, v_cache, wq, wk, wv, wo):
        import jax, jax.numpy as jnp
        import numpy as np
        import math
        DIM = 256
        B, Q_LEN, KV_LEN = (8, 128, 512)
        q = jnp.einsum('bsd,ed->bse', x, wq)
        k_new = jnp.einsum('bsd,ed->bse', x, wk)
        v_new = jnp.einsum('bsd,ed->bse', x, wv)
        k = jnp.concatenate([k_cache, k_new], axis=1)
        v = jnp.concatenate([v_cache, v_new], axis=1)
        scale = 1.0 / math.sqrt(q.shape[-1])
        scores = jnp.einsum('bqd,bkd->bqk', q, k) * scale
        attn = jax.nn.softmax(scores, axis=-1)
        out = jnp.einsum('bqk,bkd->bqd', attn, v)
        return jnp.einsum('bqd,ed->bqe', out, wo)

    def _L0_ffn_ref(hidden_states, router_w, gate_w, up_w, down_w):
        import jax, jax.numpy as jnp
        import numpy as np
        TOP_P = 0.9
        S, B, H, I, E = (256, 4, 256, 512, 8)

        def _top_p_weights(probs, top_p):
            order = jnp.argsort(-probs, axis=-1)
            sp = jnp.take_along_axis(probs, order, axis=-1)
            cum = jnp.cumsum(sp, axis=-1)
            exceed = cum > top_p
            first_idx = jnp.argmax(exceed, axis=-1)
            first = jnp.arange(probs.shape[-1])[None, :] == first_idx[:, None]
            keep = ~exceed | first
            kept = jnp.where(keep, sp, 0.0)
            t_idx = jnp.arange(probs.shape[0])[:, None]
            return jnp.zeros_like(probs).at[t_idx, order].set(kept)
        s, b, h = hidden_states.shape
        x = hidden_states.reshape(-1, h)
        probs = jax.nn.softmax(x @ router_w.T, axis=-1)
        w = _top_p_weights(probs, TOP_P)
        out = jnp.zeros_like(x)
        n_exp = router_w.shape[0]
        for e in range(n_exp):
            g = jax.nn.silu(x @ gate_w[e].T)
            u = x @ up_w[e].T
            y = g * u @ down_w[e].T
            out = out + y * w[:, e:e + 1]
        return out.reshape(s, b, h)
    x = x + _L0_xattn_ref(_layernorm(x, axis=-1), mask_BxSx4224_bf0, ctx_2048, ctx_2048, L0_xattn_wq, L0_xattn_wk, L0_xattn_wv, L0_xattn_wo)
    x = x + _L0_ffn_ref(_layernorm(x, axis=-1), L0_ffn_router_w, L0_ffn_gate_w, L0_ffn_up_w, L0_ffn_down_w)
    return x

_drawn_inputs = setup_inputs


def setup_inputs(seed=0):
    import zlib

    import numpy as np

    out = dict(_drawn_inputs(seed))
    spreads = {}
    factors = {'L0_xattn_wk': 6.034,
     'L0_xattn_wv': 5.463,
     'L0_ffn_router_w': 8.0,
     'L0_ffn_gate_w': 7.013,
     'L0_ffn_up_w': 6.912,
     'L0_ffn_down_w': 6.952,
     'ctx_2048': 3.999}
    for name, (base, spread) in spreads.items():
        noise = np.random.default_rng([zlib.crc32(name.encode()), seed]).standard_normal(out[name].shape)
        drawn = base * np.exp(spread * noise) if base else spread * noise
        out[name] = jnp.asarray(drawn.astype(out[name].dtype))
    for name, factor in factors.items():
        out[name] = (out[name] * factor).astype(out[name].dtype)
    return out
```

```python
from contextlib import ExitStack

import numpy as np

import concourse.bass as bass
from concourse import mybir

F32 = mybir.dt.float32
F32R = mybir.dt.float32r
I32 = mybir.dt.int32
ALU = mybir.AluOpType
ACT = mybir.ActivationFunctionType
AXX = mybir.AxisListType.X

P = 128
B, SQ, D = 8, 56, 256
KV = 1500
E, I = 8, 512
HALF = P // 2
PAIRS = B // 2
KD = D // P
CH = 12
CP = KV // CH
SB = 3
SC = KV // SB
GC = CH // SB
BANK = 512
TOK = B * SQ
PT = 2 * SQ
IC = I // P
UNITS = E * IC
GW = KD * I
WCOLS = 2 * GW + IC * D
WPIECE = WCOLS // IC
TSLOTS, NSLOTS = 3, 4
SCALE = 1.0 / 16.0
EPS = 1e-5
TOP_P = 0.9
MASKED = -3.0e38
IDENT_STEPS, CONSTS = 2, 10


def build(nc, x, wproj, rw, ctx_t, ctx_n, wffn, out):
    with ExitStack() as ctx:
        def sb(name, shape, dt=F32):
            return ctx.enter_context(nc.sbuf_tensor(name, shape, dt))

        def pb(name, cols):
            return ctx.enter_context(nc.psum_tensor(name, [P, cols], F32))

        def sem(name):
            return ctx.enter_context(nc.semaphore(name))

        scores = pb("scores", SB * BANK)
        tail = pb("tail", BANK)
        ptb = [pb(f"ptb{i}", BANK) for i in range(2)]
        ob = pb("ob", BANK)
        mb = pb("mb", BANK)
        gate_ps = [scores[:, 0:TOK], scores[:, 2 * BANK:2 * BANK + TOK]]
        up_ps = [scores[:, BANK:BANK + TOK], tail[:, 0:TOK]]
        y_ps = [ptb[0][:, 0:TOK], ptb[1][:, 0:TOK]]
        wb_ps = ob[:, 0:TOK]

        ring = [sb(f"ring{i}", [P, WCOLS]) for i in range(TSLOTS)]
        rows = [sb(f"rows{i}", [P, CH * D]) for i in range(NSLOTS)]
        whi = [sb(f"whi{i}", [P, WCOLS], F32R) for i in range(2)]
        wlo = [sb(f"wlo{i}", [P, WCOLS], F32R) for i in range(2)]
        x0 = sb("x0", [P, PAIRS, D])
        x1 = sb("x1", [P, PAIRS, D])
        xn = sb("xn", [P, PAIRS, D])
        xnT = sb("xnT", [P, KD, PAIRS * P])
        qT = sb("qT", [P, KD, PAIRS * P])
        kT = sb("kT", [P, KD, PAIRS * P])
        vn = sb("vn", [P, PAIRS, D])
        wp = sb("wp", [P, 4, KD, D])
        rws = sb("rws", [P, KD, E])
        probs = sb("probs", [P, KV + P])
        probsT = sb("probsT", [P, (CH + 1) * P])
        tails = sb("tails", [P, P])
        on = sb("on", [P, D])
        oT = sb("oT", [P, D])
        x2T = sb("x2T", [P, KD, P])
        x2hi = sb("x2hi", [P, KD, TOK], F32R)
        x2lo = sb("x2lo", [P, KD, TOK], F32R)
        hhi = [sb(f"hhi{i}", [P, TOK], F32R) for i in range(2)]
        hlo = [sb(f"hlo{i}", [P, TOK], F32R) for i in range(2)]
        ident = sb("ident", [P, P])
        mask = sb("mask", [P, P])
        below = sb("below", [P, E, E])
        self32 = x1[0:2 * E, :, :].rearrange("r n d -> r (n d)").rearrange("r (e m) -> r e m", e=E)
        sel = sb("sel", [2 * E, E, P], F32R)
        w16 = sb("w16", [P, PAIRS, 2 * E], F32R)
        w16T = sb("w16T", [2 * E, TOK], F32R)
        stats = sb("stats", [P, PAIRS, 6])
        mv = sb("mv", [P, PAIRS, 2])
        nr = sb("nr", [P, 4, PAIRS])
        mx = sb("mx", [P, 4 * PAIRS])
        nm = sb("nm", [P, PAIRS])
        rs = sb("rs", [P, 4 * PAIRS])
        rsum = sb("rsum", [P, PAIRS])
        rinv = sb("rinv", [P, PAIRS])
        rt = sb("rt", [P, PAIRS, 8])
        pr = sb("pr", [P, PAIRS, E])
        rex = sb("rex", [P, E])
        sil = [rows[0][:, i * BANK:i * BANK + TOK] for i in range(2)]
        sw = [rows[0][:, (2 + i) * BANK:(2 + i) * BANK + TOK] for i in range(2)]
        hid = [rows[0][:, (4 + i) * BANK:(4 + i) * BANK + TOK] for i in range(2)]
        wbs = [rows[1][:, i * BANK:i * BANK + TOK] for i in range(2)]
        fin = rows[1][:, 2 * BANK:2 * BANK + PAIRS * D].rearrange("p (n d) -> p n d", n=PAIRS)
        cmp = sb("cmp", [P, 3, E, E])

        x_in, wp_in, rw_in = sem("x_in"), sem("wp_in"), sem("rw_in")
        ring_in = [sem(f"ring_in{i}") for i in range(TSLOTS)]
        rows_in = [sem(f"rows_in{i}") for i in range(NSLOTS)]
        consts_ready, sel_ready = sem("consts_ready"), sem("sel_ready")
        dve_step = sem("dve_step")
        xn_ready, xnT_ps, xnT_act, xnT_dve = sem("xn_ready"), sem("xnT_ps"), sem("xnT_act"), sem("xnT_dve")
        proj_ps, proj_act, proj_dve = sem("proj_ps"), sem("proj_act"), sem("proj_dve")
        score_ps, negmax_ready, exp_done = sem("score_ps"), sem("negmax_ready"), sem("exp_done")
        pt_ps, pt_act, pt_dve, pv_ps = sem("pt_ps"), sem("pt_act"), sem("pt_dve"), sem("pv_ps")
        on_ready, oT_ps, oT_ready, wo_ps = sem("on_ready"), sem("oT_ps"), sem("oT_ready"), sem("wo_ps")
        x1_ready, xn2_ready, x2T_ps = sem("x1_ready"), sem("xn2_ready"), sem("x2T_ps")
        x2f_ready, x2hi_ready, x2lo_ready = sem("x2f_ready"), sem("x2hi_ready"), sem("x2lo_ready")
        logit_ps, rmax_ready, rexp_done, w16_ready = sem("logit_ps"), sem("rmax_ready"), sem("rexp_done"), sem("w16_ready")
        w16T_ps, w16T_ready, wb_ps_ready, wb_ready = sem("w16T_ps"), sem("w16T_ready"), sem("wb_ps_ready"), sem("wb_ready")
        gate_ready, up_ready, silu_done = sem("gate_ready"), sem("up_ready"), sem("silu_done")
        sw_done, hid_done, hhi_done, hlo_done = sem("sw_done"), sem("hid_done"), sem("hhi_done"), sem("hlo_done")
        whi_done, wlo0_done, wlo_done, down_done = sem("whi_done"), sem("wlo0_done"), sem("wlo_done"), sem("down_done")
        yT_act, yT_dve, y_ps_ready, fin_ready = sem("yT_act"), sem("yT_dve"), sem("y_ps_ready"), sem("fin_ready")
        out_done = sem("out_done")

        block = ctx.enter_context(nc.Block())

        def score_bank(j):
            return scores[:, j * BANK:j * BANK + SC]

        def ring_arrived(eng, item):
            eng.wait_ge(ring_in[item % TSLOTS], 16 * (item // TSLOTS + 1))

        def rows_arrived(eng, b):
            eng.wait_ge(rows_in[b % NSLOTS], 16 * (b // NSLOTS + 1))

        def halves(ap):
            return ap.rearrange("p k (h s) -> p k h s", h=2)[:, :, :, 0:SQ]

        def wcol(e, j):
            g = [slice(k * I + j * P, k * I + (j + 1) * P) for k in range(KD)]
            u = [slice(GW + k * I + j * P, GW + k * I + (j + 1) * P) for k in range(KD)]
            d = [slice(2 * GW + j * D + m * P, 2 * GW + j * D + (m + 1) * P) for m in range(KD)]
            return g, u, d

        @block.sync
        def _(sp):
            sp.dma_start(x0[:, :, :], x).then_inc(x_in, 16)
            sp.dma_start(wp[:, :, :, :], wproj).then_inc(wp_in, 16)
            sp.dma_start(rws[:, :, :], rw).then_inc(rw_in, 16)
            for n in range(PAIRS):
                for b in (2 * n, 2 * n + 1):
                    if b >= TSLOTS:
                        sp.wait_ge(score_ps, (SB + 1) * ((b - TSLOTS) // 2 + 1))
                    sp.dma_start(ring[b % TSLOTS][:, 0:KD * KV], ctx_t[b]).then_inc(ring_in[b % TSLOTS], 16)
                for b in (2 * n, 2 * n + 1):
                    if b >= NSLOTS:
                        sp.wait_ge(pv_ps, (b - NSLOTS) // 2 + 1)
                    sp.dma_start(rows[b % NSLOTS][:, :], ctx_n[b]).then_inc(rows_in[b % NSLOTS], 16)
            for e in range(E):
                item = B + e
                if e < TSLOTS:
                    sp.wait_ge(score_ps, (SB + 1) * ((item - TSLOTS) // 2 + 1))
                else:
                    sp.wait_ge(whi_done, IC * (e - TSLOTS + 1))
                    if e == TSLOTS:
                        sp.wait_ge(wlo0_done, IC)
                    else:
                        sp.wait_ge(wlo_done, IC * (e - TSLOTS))
                sp.dma_start(ring[item % TSLOTS][:, :], wffn[e]).then_inc(ring_in[item % TSLOTS], 16)
            for n in range(PAIRS):
                sp.wait_ge(fin_ready, n + 1)
                sp.dma_start(out[2 * n], fin[0:SQ, n, :]).then_inc(out_done, 16)
            sp.wait_ge(out_done, 16 * B)

        @block.gpsimd
        def _(pool):
            built = [0]

            def made(ins):
                built[0] += 1
                ins.then_inc(consts_ready, 1)
                pool.wait_ge(consts_ready, built[0])

            made(pool.memset(ident[:, :], 0.0))
            made(pool.affine_select(out=ident[:, :], in_=ident[:, :], compare_op=ALU.not_equal, fill=1.0, base=0,
                                    pattern=[[-1, P]], channel_multiplier=1))
            made(pool.memset(mask[:, :], MASKED))
            made(pool.memset(mask[0:HALF, 0:SQ], 0.0))
            made(pool.memset(mask[HALF:P, HALF:HALF + SQ], 0.0))
            made(pool.memset(below[:, :, :], 0.0))
            made(pool.affine_select(out=below[:, :, :], in_=below[:, :, :], compare_op=ALU.is_ge, fill=1.0, base=0,
                                    pattern=[[-1, E], [1, E]], channel_multiplier=0))
            made(pool.memset(self32, 0.0))
            for part in range(2):
                made(pool.affine_select(out=self32, in_=self32, compare_op=ALU.not_equal, fill=1.0, base=-part * E,
                                        pattern=[[-1, E], [0, P]], channel_multiplier=1))
            assert built[0] == CONSTS
            ring_arrived(pool, B)
            for j in range(IC):
                pool.wait_ge(whi_done, j + 1)
                c = slice(j * WPIECE, (j + 1) * WPIECE)
                pool.tensor_tensor(wlo[0][:, c], ring[B % TSLOTS][:, c], whi[0][:, c].bitcast(F32),
                                   ALU.subtract).then_inc(wlo0_done, 1)

        @block.scalar
        def _(act):
            def split_hi(e, j):
                if j == 0:
                    ring_arrived(act, B + e)
                    if e >= 2:
                        act.wait_ge(down_done, IC * (e - 1))
                c = slice(j * WPIECE, (j + 1) * WPIECE)
                act.copy(whi[e % 2][:, c], ring[(B + e) % TSLOTS][:, c]).then_inc(whi_done, 1)

            act.wait_ge(xnT_ps, 1)
            act.copy(xnT[:, 0, :], ptb[0][:, :]).then_inc(xnT_act, 1)
            act.wait_ge(proj_ps, 1)
            act.activation(qT[:, 0, :], scores[:, 0:BANK], ACT.Copy, scale=SCALE).then_inc(proj_act, 1)
            act.wait_ge(proj_ps, 3)
            act.copy(kT[:, 0, :], scores[:, 2 * BANK:3 * BANK]).then_inc(proj_act, 1)
            act.wait_ge(proj_ps, 5)
            act.copy(vn[:, 0:2, :], ob[:, :]).then_inc(proj_act, 1)

            for m in range(PAIRS + 2):
                r, o = m - 2, m - 1
                if 0 <= r:
                    act.wait_ge(rmax_ready, r + 1)
                    act.activation(pr[:, r, :], tail[:, 2 * P:2 * P + E], ACT.Exp, bias=rt[:, r, 0:1],
                                   accum_out=rt[:, r, 1:2]).then_inc(rexp_done, 1)
                if 0 <= o < PAIRS:
                    act.wait_ge(oT_ps, o + 1)
                    if o >= 1:
                        act.wait_ge(wo_ps, o)
                    act.copy(oT[:, :], mb[:, 0:D]).then_inc(oT_ready, 1)
                if m < PAIRS:
                    n = m
                    act.wait_ge(negmax_ready, n + 1)
                    if n >= 1:
                        act.wait_ge(pt_ps, 4 * n)
                    for j in range(SB):
                        act.activation(probs[:, j * SC:(j + 1) * SC], score_bank(j), ACT.Exp, bias=nm[:, n:n + 1],
                                       accum_out=rs[:, 4 * n + j:4 * n + j + 1]).then_inc(exp_done, 1)
                    act.activation(probs[:, KV:KV + P], tails[:, :], ACT.Exp, bias=nm[:, n:n + 1],
                                   accum_out=rs[:, 4 * n + 3:4 * n + 4]).then_inc(exp_done, 1)
                    for j in (0, 2):
                        act.wait_ge(pt_ps, 4 * n + j + 1)
                        if n >= 1 and j == 0:
                            act.wait_ge(pv_ps, n)
                        act.copy(probsT[0:CP, j * BANK:(j + 1) * BANK], ptb[0][0:CP, :]).then_inc(pt_act, 1)
                if m == PAIRS - 1:
                    for j in range(IC):
                        split_hi(0, j)
                if 0 <= o < PAIRS:
                    act.wait_ge(x2T_ps, o + 1)
                    if o >= 1:
                        act.wait_ge(logit_ps, o)
                    act.copy(x2T[:, :, :], mb[:, 0:D].rearrange("p (k t) -> p k t", k=KD)).then_inc(x2f_ready, 1)
                    act.copy(x2hi[:, :, o * PT:(o + 1) * PT].rearrange("p k (h s) -> p k h s", h=2),
                             halves(mb[:, 0:D].rearrange("p (k t) -> p k t", k=KD))).then_inc(x2hi_ready, 1)

            act.wait_ge(w16T_ps, 1)
            act.copy(w16T[:, :].rearrange("r (n h s) -> r n h s", n=PAIRS, h=2),
                     halves(mb[0:2 * E, :].rearrange("r (n t) -> r n t", n=PAIRS))).then_inc(w16T_ready, 1)
            act.wait_ge(wb_ps_ready, 1)
            act.copy(wbs[0], wb_ps).then_inc(wb_ready, 1)

            for e in range(E):
                for j in range(IC):
                    u = IC * e + j
                    act.wait_ge(gate_ready, u + 1)
                    if u >= 2:
                        act.wait_ge(sw_done, u - 1)
                    act.activation(sil[u % 2], gate_ps[u % 2], ACT.Silu).then_inc(silu_done, 1)
                    act.wait_ge(hid_done, u + 1)
                    if u >= 2:
                        act.wait_ge(down_done, u - 1)
                    act.copy(hhi[u % 2][:, :], hid[u % 2]).then_inc(hhi_done, 1)
                    if e + 1 < E:
                        split_hi(e + 1, j)
                        if j == 2:
                            act.wait_ge(wb_ps_ready, e + 2)
                            if e >= 1:
                                act.wait_ge(sw_done, IC * e)
                            act.copy(wbs[(e + 1) % 2], wb_ps).then_inc(wb_ready, 1)

            act.wait_ge(down_done, UNITS)
            act.copy(halves(xnT[:, 0, :].rearrange("p (n t) -> p n t", n=PAIRS)),
                     y_ps[0].rearrange("p (n h s) -> p n h s", n=PAIRS, h=2)).then_inc(yT_act, 1)
            for n in range(PAIRS):
                act.wait_ge(fin_ready, n + 1)
                act.dma_start(out[2 * n + 1], fin[HALF:HALF + SQ, n, :]).then_inc(out_done, 16)
            act.wait_ge(out_done, 16 * B)

        @block.vector
        def _(dve):
            steps = [0]

            def link(ins):
                steps[0] += 1
                ins.then_inc(dve_step, 1)
                dve.wait_ge(dve_step, steps[0])

            def layernorm(src, lo, hi, ready):
                for n in range(lo, hi):
                    link(dve.bn_stats(stats[:, n, :], src[:, n, :]))
                    link(dve.bn_aggr(mv[:, n, :], stats[:, n, :]))
                ve, y, a, b = (nr[:, i, lo:hi] for i in range(4))
                link(dve.tensor_scalar(ve, mv[:, lo:hi, 1], EPS, None, ALU.add))
                link(dve.tensor_scalar(y.bitcast(I32), ve.bitcast(I32), -0.5, float(0x5F3759DF), ALU.mult, ALU.add))
                for _ in range(4):
                    link(dve.tensor_tensor(a, y, y, ALU.mult))
                    link(dve.scalar_tensor_tensor(b, a, -0.5, ve, ALU.mult, ALU.mult))
                    link(dve.scalar_tensor_tensor(y, b, 1.5, y, ALU.add, ALU.mult))
                for n in range(lo, hi):
                    dve.tensor_scalar(xn[:, n, :], src[:, n, :], mv[:, n, 0:1], y[:, n - lo:n - lo + 1],
                                      ALU.subtract, ALU.mult).then_inc(ready, 1)

            dve.wait_ge(x_in, 16)
            layernorm(x0, 0, PAIRS, xn_ready)
            dve.wait_ge(xnT_ps, 2)
            dve.tensor_copy(xnT[:, 1, :], ptb[1][:, :]).then_inc(xnT_dve, 1)
            dve.wait_ge(proj_ps, 2)
            dve.tensor_scalar(qT[:, 1, :], scores[:, BANK:2 * BANK], SCALE, None, ALU.mult).then_inc(proj_dve, 1)
            dve.wait_ge(proj_ps, 4)
            dve.tensor_copy(kT[:, 1, :], tail[:, :]).then_inc(proj_dve, 1)
            dve.wait_ge(proj_ps, 6)
            dve.tensor_copy(vn[:, 2:4, :], mb[:, :]).then_inc(proj_dve, 1)
            dve.wait_ge(consts_ready, CONSTS)
            dve.tensor_copy(sel[:, :, :], self32).then_inc(sel_ready, 1)

            def router_max(r):
                dve.wait_ge(logit_ps, r + 1)
                dve.tensor_reduce(rt[:, r, 0:1], tail[:, 2 * P:2 * P + E], AXX, ALU.max,
                                  negate=True).then_inc(rmax_ready, 1)

            def router_weights(r):
                dve.wait_ge(rexp_done, r + 1)
                p = pr[:, r, :]
                link(dve.reciprocal(rt[:, r, 2:3], rt[:, r, 1:2]))
                link(dve.tensor_scalar(p, p, rt[:, r, 2:3], None, ALU.mult))
                pf = p.rearrange("q (a f) -> q a f", a=1).broadcast_to([P, E, E])
                pe = p.rearrange("q (f a) -> q f a", a=1).broadcast_to([P, E, E])
                link(dve.tensor_tensor(cmp[:, 0], pf, pe, ALU.is_gt))
                link(dve.tensor_tensor(cmp[:, 1], pf, pe, ALU.is_equal))
                link(dve.tensor_tensor(cmp[:, 2], cmp[:, 1], below[:, :, :], ALU.mult))
                link(dve.tensor_tensor(cmp[:, 1], cmp[:, 0], cmp[:, 2], ALU.add))
                link(dve.tensor_tensor(cmp[:, 0], cmp[:, 1], pf, ALU.mult))
                link(dve.tensor_reduce(rex[:, :], cmp[:, 0], AXX, ALU.add))
                link(dve.scalar_tensor_tensor(cmp[:, 1, 0, :], rex[:, :], TOP_P, p, ALU.is_le, ALU.mult))
                link(dve.tensor_copy(w16[:, r, 0:E], cmp[:, 1, 0, :]))
                dve.tensor_tensor(w16[:, r, E:2 * E], cmp[:, 1, 0, :], w16[:, r, 0:E].bitcast(F32),
                                  ALU.subtract).then_inc(w16_ready, 1)

            for m in range(PAIRS + 2):
                r, o = m - 2, m - 1
                if 0 <= r:
                    router_max(r)
                if m < PAIRS:
                    n = m
                    for j in range(SB):
                        dve.wait_ge(score_ps, 4 * n + j + 1)
                        dve.tensor_reduce(mx[:, 4 * n + j:4 * n + j + 1], score_bank(j), AXX, ALU.max)
                    dve.wait_ge(score_ps, 4 * n + 4)
                    if n >= 1:
                        dve.wait_ge(exp_done, 4 * n)
                    link(dve.tensor_tensor(tails[:, :], tail[:, 0:P], mask[:, :], ALU.add))
                    link(dve.tensor_reduce(mx[:, 4 * n + 3:4 * n + 4], tails[:, :], AXX, ALU.max))
                    dve.tensor_reduce(nm[:, n:n + 1], mx[:, 4 * n:4 * n + 4], AXX, ALU.max,
                                      negate=True).then_inc(negmax_ready, 1)
                    dve.wait_ge(pt_ps, 4 * n + 2)
                    if n >= 1:
                        dve.wait_ge(pv_ps, n)
                    dve.tensor_copy(probsT[0:CP, BANK:2 * BANK], ptb[1][0:CP, :]).then_inc(pt_dve, 1)
                    dve.wait_ge(pt_ps, 4 * n + 4)
                    dve.tensor_copy(probsT[:, CH * P:(CH + 1) * P], ptb[1][:, 0:P]).then_inc(pt_dve, 1)
                if 0 <= o < PAIRS:
                    dve.wait_ge(wo_ps, o + 1)
                    dve.tensor_tensor(x1[:, o, :], x0[:, o, :], mb[:, D:2 * D], ALU.add).then_inc(x1_ready, 1)
                    dve.wait_ge(x1_ready, o + 1)
                    layernorm(x1, o, o + 1, xn2_ready)
                if 0 <= r:
                    router_weights(r)
                if m < PAIRS:
                    n = m
                    dve.wait_ge(exp_done, 4 * n + 4)
                    link(dve.tensor_reduce(rsum[:, n:n + 1], rs[:, 4 * n:4 * n + 4], AXX, ALU.add))
                    link(dve.reciprocal(rinv[:, n:n + 1], rsum[:, n:n + 1]))
                    dve.wait_ge(pv_ps, n + 1)
                    if n >= 1:
                        dve.wait_ge(oT_ps, n)
                    dve.tensor_scalar(on[:, :], ob[:, 0:D], rinv[:, n:n + 1], None, ALU.mult).then_inc(on_ready, 1)
                if 0 <= o < PAIRS:
                    dve.wait_ge(x2hi_ready, o + 1)
                    dve.tensor_tensor(x2lo[:, :, o * PT:(o + 1) * PT].rearrange("p k (h s) -> p k h s", h=2),
                                      halves(mb[:, 0:D].rearrange("p (k t) -> p k t", k=KD)),
                                      x2hi[:, :, o * PT:(o + 1) * PT].bitcast(F32).rearrange("p k (h s) -> p k h s", h=2),
                                      ALU.subtract).then_inc(x2lo_ready, 1)

            for e in range(E):
                for j in range(IC):
                    u = IC * e + j
                    if j == 0:
                        dve.wait_ge(wb_ready, e + 1)
                    dve.wait_ge(silu_done, u + 1)
                    dve.tensor_tensor(sw[u % 2], sil[u % 2], wbs[e % 2], ALU.mult).then_inc(sw_done, 1)
                    dve.wait_ge(sw_done, u + 1)
                    dve.wait_ge(up_ready, u + 1)
                    dve.tensor_tensor(hid[u % 2], sw[u % 2], up_ps[u % 2], ALU.mult).then_inc(hid_done, 1)
                    dve.wait_ge(hhi_done, u + 1)
                    if u >= 2:
                        dve.wait_ge(down_done, u - 1)
                    dve.tensor_tensor(hlo[u % 2][:, :], hid[u % 2], hhi[u % 2][:, :].bitcast(F32),
                                      ALU.subtract).then_inc(hlo_done, 1)
                    if e + 1 < E:
                        dve.wait_ge(whi_done, IC * (e + 1) + j + 1)
                        c = slice(j * WPIECE, (j + 1) * WPIECE)
                        dve.tensor_tensor(wlo[(e + 1) % 2][:, c], ring[(B + e + 1) % TSLOTS][:, c],
                                          whi[(e + 1) % 2][:, c].bitcast(F32), ALU.subtract).then_inc(wlo_done, 1)

            dve.wait_ge(down_done, UNITS)
            dve.tensor_copy(halves(xnT[:, 1, :].rearrange("p (n t) -> p n t", n=PAIRS)),
                            y_ps[1].rearrange("p (n h s) -> p n h s", n=PAIRS, h=2)).then_inc(yT_dve, 1)
            for n in range(PAIRS):
                src = (scores[:, n * BANK:n * BANK + D] if n < SB else tail[:, 0:D])
                dve.wait_ge(y_ps_ready, n + 1)
                dve.tensor_tensor(fin[:, n, :], x1[:, n, :], src, ALU.add).then_inc(fin_ready, 1)

        @block.tensor
        def _(pe):
            mm = nc.tensor.matmul

            def transpose(dst, src, last=None):
                ins = nc.tensor.transpose(dst, src, ident[0:src.shape[0], 0:src.shape[0]])
                if last is not None:
                    ins.then_inc(last, 1)

            pe.wait_ge(consts_ready, IDENT_STEPS)
            pe.wait_ge(xn_ready, PAIRS)
            for k in range(KD):
                for n in range(PAIRS):
                    transpose(ptb[k][:, n * P:(n + 1) * P], xn[:, n, k * P:(k + 1) * P],
                              xnT_ps if n == PAIRS - 1 else None)
            pe.wait_ge(wp_in, 16)
            pe.wait_ge(xnT_act, 1)
            pe.wait_ge(xnT_dve, 1)
            for i, (w, m) in enumerate([(0, 0), (0, 1), (1, 0), (1, 1)]):
                dst = scores[:, i * BANK:(i + 1) * BANK] if i < SB else tail[:, :]
                for k in range(KD):
                    ins = mm(dst, wp[:, w, k, m * P:(m + 1) * P], xnT[:, k, :], start=k == 0, stop=k == KD - 1)
                ins.then_inc(proj_ps, 1)
            for n in range(PAIRS):
                dst = (ob if n < 2 else mb)[:, (n % 2) * D:(n % 2 + 1) * D]
                for k in range(KD):
                    ins = mm(dst, xnT[:, k, n * P:(n + 1) * P], wp[:, 2, k, :], start=k == 0, stop=k == KD - 1)
                if n % 2:
                    ins.then_inc(proj_ps, 1)

            def logits(r):
                pe.wait_ge(x2f_ready, r + 1)
                if r == 0:
                    pe.wait_ge(rw_in, 16)
                for k in range(KD):
                    ins = mm(tail[:, 2 * P:2 * P + E], x2T[:, k, :], rws[:, k, :], start=k == 0, stop=k == KD - 1)
                ins.then_inc(logit_ps, 1)

            def gate_up(u):
                e, j = u // IC, u % IC
                g, up, _ = wcol(e, j)
                if j == 0:
                    pe.wait_ge(whi_done, IC * (e + 1))
                    if e == 0:
                        pe.wait_ge(wlo0_done, IC)
                    else:
                        pe.wait_ge(wlo_done, IC * e)
                for dst, cols, ready, freed in ((gate_ps, g, gate_ready, silu_done), (up_ps, up, up_ready, hid_done)):
                    if u >= 2:
                        pe.wait_ge(freed, u - 1)
                    n = 0
                    for k in range(KD):
                        for w, xx in ((whi, x2hi), (whi, x2lo), (wlo, x2hi)):
                            ins = mm(dst[u % 2], w[e % 2][:, cols[k]], xx[:, k, :], start=n == 0, stop=n == 3 * KD - 1)
                            n += 1
                    ins.then_inc(ready, 1)

            def down(u):
                e, j = u // IC, u % IC
                _, _, d = wcol(e, j)
                pe.wait_ge(hhi_done, u + 1)
                pe.wait_ge(hlo_done, u + 1)
                for m in range(KD):
                    for i, (w, h) in enumerate(((whi, hhi), (whi, hlo), (wlo, hhi))):
                        ins = mm(y_ps[m], w[e % 2][:, d[m]], h[u % 2][:, :], start=u == 0 and i == 0,
                                 stop=u == UNITS - 1 and i == 2)
                ins.then_inc(down_done, 1)

            def weight_rows(e):
                if e >= 1:
                    pe.wait_ge(wb_ready, e)
                mm(wb_ps, sel[:, e, :], w16T[:, :], start=True, stop=True).then_inc(wb_ps_ready, 1)

            for m in range(PAIRS + 2):
                r, o = m - 2, m - 1
                if 0 <= r:
                    logits(r)
                if m < PAIRS:
                    n = m
                    if n == 0:
                        pe.wait_ge(proj_act, 3)
                        pe.wait_ge(proj_dve, 3)
                    else:
                        pe.wait_ge(exp_done, 4 * n - 1)
                    ring_arrived(pe, 2 * n)
                    ring_arrived(pe, 2 * n + 1)
                    for j in range(SB):
                        for k in range(KD):
                            for h in range(2):
                                ins = mm(scores[h * HALF:(h + 1) * HALF, j * BANK:j * BANK + SC],
                                         qT[:, k, n * P + h * HALF:n * P + (h + 1) * HALF],
                                         ring[(2 * n + h) % TSLOTS][:, k * KV + j * SC:k * KV + (j + 1) * SC],
                                         start=k == 0, stop=k == KD - 1, tile_position=(0, h * HALF))
                        ins.then_inc(score_ps, 1)
                    if n >= 1:
                        pe.wait_ge(negmax_ready, n)
                    if 0 <= r:
                        pe.wait_ge(rexp_done, r + 1)
                    for k in range(KD):
                        ins = mm(tail[:, 0:P], qT[:, k, n * P:(n + 1) * P], kT[:, k, n * P:(n + 1) * P],
                                 start=k == 0, stop=k == KD - 1)
                    ins.then_inc(score_ps, 1)
                if 0 <= o < PAIRS:
                    pe.wait_ge(on_ready, o + 1)
                    if o >= 1:
                        pe.wait_ge(x2lo_ready, o)
                    for k in range(KD):
                        transpose(mb[:, k * P:(k + 1) * P], on[:, k * P:(k + 1) * P], oT_ps if k == KD - 1 else None)
                    pe.wait_ge(oT_ready, o + 1)
                    for k in range(KD):
                        ins = mm(mb[:, D:2 * D], oT[:, k * P:(k + 1) * P], wp[:, 3, k, :], start=k == 0, stop=k == KD - 1)
                    ins.then_inc(wo_ps, 1)
                if m < PAIRS:
                    n = m
                    for j in range(SB + 1):
                        g = 4 * n + j
                        pe.wait_ge(exp_done, g + 1)
                        if g >= 2:
                            pe.wait_ge(pt_dve if j % 2 else pt_act, g // 2)
                        if j < SB:
                            for i in range(GC):
                                c = GC * j + i
                                transpose(ptb[j % 2][0:CP, i * P:(i + 1) * P], probs[:, c * CP:(c + 1) * CP],
                                          pt_ps if i == GC - 1 else None)
                        else:
                            transpose(ptb[j % 2][:, 0:P], probs[:, KV:KV + P], pt_ps)
                    if n >= 1:
                        pe.wait_ge(on_ready, n)
                    for c in range(CH):
                        j = c // GC
                        if c % GC == 0:
                            if j % 2:
                                pe.wait_ge(pt_dve, 2 * n + 1)
                            else:
                                pe.wait_ge(pt_act, 2 * n + j // 2 + 1)
                        if c == 0:
                            rows_arrived(pe, 2 * n)
                            rows_arrived(pe, 2 * n + 1)
                        for h in range(2):
                            mm(ob[h * HALF:(h + 1) * HALF, 0:D], probsT[0:CP, c * P + h * HALF:c * P + (h + 1) * HALF],
                               rows[(2 * n + h) % NSLOTS][0:CP, c * D:(c + 1) * D], start=c == 0, stop=False,
                               tile_position=(0, h * HALF), skip_group_check=True)
                    pe.wait_ge(pt_dve, 2 * n + 2)
                    mm(ob[:, 0:D], probsT[:, CH * P:(CH + 1) * P], vn[:, n, :], start=False, stop=True,
                       skip_group_check=True).then_inc(pv_ps, 1)
                if 0 <= o < PAIRS:
                    pe.wait_ge(xn2_ready, o + 1)
                    for k in range(KD):
                        transpose(mb[:, k * P:(k + 1) * P], xn[:, o, k * P:(k + 1) * P], x2T_ps if k == KD - 1 else None)

            pe.wait_ge(x2lo_ready, PAIRS)
            gate_up(0)
            pe.wait_ge(w16_ready, PAIRS)
            for n in range(PAIRS):
                transpose(mb[0:2 * E, n * P:(n + 1) * P], w16[:, n, :].bitcast(F32), w16T_ps if n == PAIRS - 1 else None)
            pe.wait_ge(w16T_ready, 1)
            pe.wait_ge(sel_ready, 1)
            weight_rows(0)
            pe.wait_ge(rexp_done, PAIRS)
            for u in range(1, UNITS):
                gate_up(u)
                down(u - 1)
                if u % IC == 1 and u // IC + 1 < E:
                    weight_rows(u // IC + 1)
            down(UNITS - 1)

            pe.wait_ge(yT_act, 1)
            pe.wait_ge(yT_dve, 1)
            for n in range(PAIRS):
                dst = scores[:, n * BANK:n * BANK + D] if n < SB else tail[:, 0:D]
                for k in range(KD):
                    transpose(dst[:, k * P:(k + 1) * P], xnT[:, k, n * P:(n + 1) * P], y_ps_ready if k == KD - 1 else None)


def kernel(x, ctx_2048, mask_BxSx4224_bf0, L0_xattn_wq, L0_xattn_wk, L0_xattn_wv, L0_xattn_wo,
           L0_ffn_router_w, L0_ffn_gate_w, L0_ffn_up_w, L0_ffn_down_w):
    import concourse.bacc as bacc
    from concourse.bass_utils import run_bass_kernel_spmd

    x = np.asarray(x)
    ctx = np.asarray(ctx_2048)
    xp = np.zeros((2, HALF, PAIRS, D), x.dtype)
    xp[:, :SQ] = x.reshape(PAIRS, 2, SQ, D).transpose(1, 2, 0, 3)
    proj = np.stack([np.asarray(w).T.reshape(KD, P, D).transpose(1, 0, 2)
                     for w in (L0_xattn_wq, L0_xattn_wk, L0_xattn_wv, L0_xattn_wo)], axis=1)
    router = np.asarray(L0_ffn_router_w).T.reshape(KD, P, E).transpose(1, 0, 2)
    ctx_t = ctx.reshape(B, CP, CH, KD, P).transpose(0, 4, 3, 2, 1).reshape(B, P, KD * KV)
    ctx_n = np.zeros((B, P, CH * D), ctx.dtype)
    ctx_n[:, :CP] = ctx.reshape(B, CP, CH * D)

    def width_first(w):
        return np.asarray(w).transpose(0, 2, 1).reshape(E, KD, P, I).transpose(0, 2, 1, 3).reshape(E, P, GW)

    down = np.asarray(L0_ffn_down_w).transpose(0, 2, 1).reshape(E, IC, P, D).transpose(0, 2, 1, 3).reshape(E, P, IC * D)
    wffn = np.concatenate([width_first(L0_ffn_gate_w), width_first(L0_ffn_up_w), down], axis=2)

    arrays = {"xp": xp.reshape(P, PAIRS, D), "wproj": proj, "router": router,
              "ctx_t": ctx_t, "ctx_n": ctx_n, "wffn": wffn}
    arrays = {k: np.ascontiguousarray(v) for k, v in arrays.items()}
    nc = bacc.Bacc("TRN2", target_bir_lowering=False, num_devices=1)
    args = [nc.dram_tensor(k, v.shape, mybir.dt.from_np(v.dtype), kind="ExternalInput").ap() for k, v in arrays.items()]
    args.append(nc.dram_tensor("out", (B, SQ, D), F32, kind="ExternalOutput").ap())
    build(nc, *args)
    result = run_bass_kernel_spmd(nc, [arrays], core_ids=[0])
    return result.results[0]["out"]
```

```python
from contextlib import ExitStack

import numpy as np

import concourse.bass as bass
from concourse import mybir

F32 = mybir.dt.float32
F32R = mybir.dt.float32r
I32 = mybir.dt.int32
ALU = mybir.AluOpType
ACT = mybir.ActivationFunctionType
AXX = mybir.AxisListType.X

P = 128
B, SQ, D = 8, 56, 256
KV = 1500
E, I = 8, 512
HALF = P // 2
PAIRS = B // 2
KD = D // P
CH = 12
CP = KV // CH
SB = 3
SC = KV // SB
GC = CH // SB
BANK = 512
TOK = B * SQ
PT = 2 * SQ
IC = I // P
UNITS = E * IC
GW = KD * I
WCOLS = 2 * GW + IC * D
PIECES = [slice(j * WCOLS // IC, (j + 1) * WCOLS // IC) for j in range(IC)]
EARLY = 3
TSLOTS, NSLOTS = 3, 4
HT = TOK // 2
SCALE = 1.0 / 16.0
EPS = 1e-5
TOP_P = 0.9
MASKED = -3.0e38
IDENT_STEPS, CONSTS = 2, 10


def build(nc, x, wproj, rw, ctx_t, ctx_n, wffn, out):
    with ExitStack() as ctx:
        def sb(name, shape, dt=F32):
            return ctx.enter_context(nc.sbuf_tensor(name, shape, dt))

        def pb(name, cols):
            return ctx.enter_context(nc.psum_tensor(name, [P, cols], F32))

        def sem(name):
            return ctx.enter_context(nc.semaphore(name))

        scores = pb("scores", SB * BANK)
        tail = pb("tail", BANK)
        ptb = [pb(f"ptb{i}", BANK) for i in range(2)]
        ob = pb("ob", BANK)
        mb = pb("mb", BANK)
        gate_ps = [scores[:, 0:TOK], scores[:, 2 * BANK:2 * BANK + TOK]]
        up_ps = [scores[:, BANK:BANK + TOK], ob[:, 0:TOK]]
        y_ps = [ptb[0][:, 0:TOK], ptb[1][:, 0:TOK]]
        wb_ps = tail[:, 0:TOK]
        x2T_cols = tail[:, P:3 * P].rearrange("p (k t) -> p k t", k=KD)
        xnT_banks = [ptb, [scores[:, 2 * BANK:3 * BANK], tail]]
        logit_cols = tail[:, 3 * P:3 * P + E]

        ring = [sb(f"ring{i}", [P, WCOLS]) for i in range(TSLOTS)]
        rows = [sb(f"rows{i}", [P, CH * D]) for i in range(NSLOTS)]
        whi = [sb(f"whi{i}", [P, WCOLS], F32R) for i in range(2)]
        wlo = [sb(f"wlo{i}", [P, WCOLS], F32R) for i in range(2)]
        x0 = sb("x0", [P, PAIRS, D])
        x1 = sb("x1", [P, PAIRS, D])
        xn = sb("xn", [P, PAIRS, D])
        xnT = sb("xnT", [P, KD, PAIRS * P])
        qT = sb("qT", [P, KD, PAIRS * P])
        kT = sb("kT", [P, KD, PAIRS * P])
        vn = sb("vn", [P, PAIRS, D])
        wp = sb("wp", [P, 4, KD, D])
        rws = sb("rws", [P, KD, E])
        probs = sb("probs", [P, KV + P])
        probsT = sb("probsT", [P, (CH + 1) * P])
        tails = sb("tails", [P, P])
        on = sb("on", [P, D])
        oT = sb("oT", [P, D])
        x2T = sb("x2T", [P, KD, P])
        x2hi = sb("x2hi", [P, KD, TOK], F32R)
        x2lo = sb("x2lo", [P, KD, TOK], F32R)
        hhi = [sb(f"hhi{i}", [P, TOK], F32R) for i in range(2)]
        hlo = [sb(f"hlo{i}", [P, TOK], F32R) for i in range(2)]
        ident = sb("ident", [P, P])
        mask = sb("mask", [P, P])
        below = sb("below", [P, E, E])
        self32 = x1[0:2 * E, :, :].rearrange("r n d -> r (n d)").rearrange("r (e m) -> r e m", e=E)
        sel = sb("sel", [2 * E, E, P], F32R)
        w16 = sb("w16", [P, PAIRS, 2 * E], F32R)
        w16T = sb("w16T", [2 * E, TOK], F32R)
        stats = sb("stats", [P, PAIRS, 6])
        mv = sb("mv", [P, PAIRS, 2])
        nr = sb("nr", [P, 5, PAIRS])
        mx = sb("mx", [P, 4 * PAIRS])
        nm = sb("nm", [P, PAIRS])
        rs = sb("rs", [P, 4 * PAIRS])
        rsum = sb("rsum", [P, PAIRS])
        rinv = sb("rinv", [P, PAIRS])
        rt = sb("rt", [P, PAIRS, 8])
        pr = sb("pr", [P, PAIRS, E])
        rex = sb("rex", [P, E])
        sil = [rows[0][:, i * BANK:i * BANK + TOK] for i in range(2)]
        sw = [rows[0][:, (2 + i) * BANK:(2 + i) * BANK + TOK] for i in range(2)]
        hid = [rows[0][:, (4 + i) * BANK:(4 + i) * BANK + TOK] for i in range(2)]
        wbs = [rows[1][:, i * BANK:i * BANK + TOK] for i in range(2)]
        fin = rows[1][:, 2 * BANK:2 * BANK + PAIRS * D].rearrange("p (n d) -> p n d", n=PAIRS)
        cmp = sb("cmp", [P, 3, E, E])
        before = sb("before", [P, E, 2, E])
        pn = sb("pn", [P, E])
        rw8 = sb("rw8", [P, E])

        x_in, wp_in, rw_in = sem("x_in"), sem("wp_in"), sem("rw_in")
        ring_in = [sem(f"ring_in{i}") for i in range(TSLOTS)]
        rows_in = [sem(f"rows_in{i}") for i in range(NSLOTS)]
        consts_ready, sel_ready = sem("consts_ready"), sem("sel_ready")
        dve_step = sem("dve_step")
        xn_ready, xnT_ps, xnT_act, xnT_dve = sem("xn_ready"), sem("xnT_ps"), sem("xnT_act"), sem("xnT_dve")
        proj_ps, proj_act, proj_dve = sem("proj_ps"), sem("proj_act"), sem("proj_dve")
        score_ps, tail_ps, negmax_ready, exp_done = sem("score_ps"), sem("tail_ps"), sem("negmax_ready"), sem("exp_done")
        pt_ps, pt_act, pt_dve, pv_ps = sem("pt_ps"), sem("pt_act"), sem("pt_dve"), sem("pv_ps")
        on_ready, oT_ps, oT_ready, wo_ps = sem("on_ready"), sem("oT_ps"), sem("oT_ready"), sem("wo_ps")
        x1_ready, xn2_ready, x2T_ps = sem("x1_ready"), sem("xn2_ready"), sem("x2T_ps")
        x2f_ready, x2hi_ready, x2lo_ready = sem("x2f_ready"), sem("x2hi_ready"), sem("x2lo_ready")
        logit_ps, rmax_ready, rexp_done, w16_ready = sem("logit_ps"), sem("rmax_ready"), sem("rexp_done"), sem("w16_ready")
        w16T_ps, w16T_ready, wb_ps_ready, wb_ready = sem("w16T_ps"), sem("w16T_ready"), sem("wb_ps_ready"), sem("wb_ready")
        gate_ready, up_ready, silu_done = sem("gate_ready"), sem("up_ready"), sem("silu_done")
        sw_done, hid_done, hhi_done, hlo_done = sem("sw_done"), sem("hid_done"), sem("hhi_done"), sem("hlo_done")
        whi_done, wlo0_done, wlo_done, down_done = sem("whi_done"), sem("wlo0_done"), sem("wlo_done"), sem("down_done")
        yT_act, yT_dve, y_ps_ready, fin_ready = sem("yT_act"), sem("yT_dve"), sem("y_ps_ready"), sem("fin_ready")
        out_done = sem("out_done")

        block = ctx.enter_context(nc.Block())

        def score_bank(j):
            return scores[:, j * BANK:j * BANK + SC]

        def ring_arrived(eng, item):
            eng.wait_ge(ring_in[item % TSLOTS], 16 * (item // TSLOTS + 1))

        def rows_arrived(eng, b):
            eng.wait_ge(rows_in[b % NSLOTS], 16 * (b // NSLOTS + 1))

        def halves(ap):
            return ap.rearrange("p k (h s) -> p k h s", h=2)[:, :, :, 0:SQ]

        def wcol(e, j):
            g = [slice(k * I + j * P, k * I + (j + 1) * P) for k in range(KD)]
            u = [slice(GW + k * I + j * P, GW + k * I + (j + 1) * P) for k in range(KD)]
            d = [slice(2 * GW + j * D + m * P, 2 * GW + j * D + (m + 1) * P) for m in range(KD)]
            return g, u, d

        @block.sync
        def _(sp):
            sp.dma_start(x0[:, :, :], x).then_inc(x_in, 16)
            sp.dma_start(wp[:, :, :, :], wproj).then_inc(wp_in, 16)
            sp.dma_start(rws[:, :, :], rw).then_inc(rw_in, 16)
            def load_columns(b):
                if b >= TSLOTS:
                    sp.wait_ge(score_ps, SB * ((b - TSLOTS) // 2 + 1))
                sp.dma_start(ring[b % TSLOTS][:, 0:KD * KV], ctx_t[b]).then_inc(ring_in[b % TSLOTS], 16)

            def load_rows(b):
                if b >= NSLOTS:
                    sp.wait_ge(pv_ps, (b - NSLOTS) // 2 + 1)
                sp.dma_start(rows[b % NSLOTS][:, :], ctx_n[b]).then_inc(rows_in[b % NSLOTS], 16)

            for m in range(PAIRS + 1):
                for b in (2 * m, 2 * m + 1):
                    if m < PAIRS:
                        load_columns(b)
                for b in (2 * m - 2, 2 * m - 1):
                    if m >= 1:
                        load_rows(b)
            for e in range(E):
                item = B + e
                if e < TSLOTS:
                    sp.wait_ge(score_ps, SB * ((item - TSLOTS) // 2 + 1))
                else:
                    sp.wait_ge(whi_done, IC * (e - TSLOTS + 1))
                    if e == TSLOTS:
                        sp.wait_ge(wlo0_done, IC)
                    else:
                        sp.wait_ge(wlo_done, IC * (e - TSLOTS))
                sp.dma_start(ring[item % TSLOTS][:, :], wffn[e]).then_inc(ring_in[item % TSLOTS], 16)
            out_v = out.rearrange("(n h) s d -> h s n d", h=2)
            for n in (0, 2):
                sp.wait_ge(fin_ready, n + 2)
                sp.dma_start(out_v[0, :, n:n + 2, :], fin[0:SQ, n:n + 2, :]).then_inc(out_done, 16)
            sp.wait_ge(out_done, 16 * PAIRS)

        @block.gpsimd
        def _(pool):
            built = [0]

            def made(ins):
                built[0] += 1
                ins.then_inc(consts_ready, 1)
                pool.wait_ge(consts_ready, built[0])

            made(pool.memset(ident[:, :], 0.0))
            made(pool.affine_select(out=ident[:, :], in_=ident[:, :], compare_op=ALU.not_equal, fill=1.0, base=0,
                                    pattern=[[-1, P]], channel_multiplier=1))
            made(pool.memset(mask[:, :], MASKED))
            made(pool.memset(mask[0:HALF, 0:SQ], 0.0))
            made(pool.memset(mask[HALF:P, HALF:HALF + SQ], 0.0))
            made(pool.memset(below[:, :, :], 0.0))
            made(pool.affine_select(out=below[:, :, :], in_=below[:, :, :], compare_op=ALU.is_ge, fill=1.0, base=0,
                                    pattern=[[-1, E], [1, E]], channel_multiplier=0))
            made(pool.memset(self32, 0.0))
            for part in range(2):
                made(pool.affine_select(out=self32, in_=self32, compare_op=ALU.not_equal, fill=1.0, base=-part * E,
                                        pattern=[[-1, E], [0, P]], channel_multiplier=1))
            assert built[0] == CONSTS
            ring_arrived(pool, B)
            for j in range(IC):
                pool.wait_ge(whi_done, j + 1)
                c = PIECES[j]
                pool.tensor_tensor(wlo[0][:, c], ring[B % TSLOTS][:, c], whi[0][:, c].bitcast(F32),
                                   ALU.subtract).then_inc(wlo0_done, 1)

        @block.scalar
        def _(act):
            def split_hi(e, j):
                if j == 0:
                    ring_arrived(act, B + e)
                if e >= 2:
                    act.wait_ge(*((up_ready, IC * (e - 1)) if j < EARLY else (down_done, IC * (e - 1))))
                c = PIECES[j]
                act.copy(whi[e % 2][:, c], ring[(B + e) % TSLOTS][:, c]).then_inc(whi_done, 1)

            for h in range(2):
                c = slice(h * D, (h + 1) * D)
                act.wait_ge(xnT_ps, 2 * h + 1)
                act.copy(xnT[:, 0, c], xnT_banks[h][0][:, c]).then_inc(xnT_act, 1)
            for i, (dst, src) in enumerate(((qT[:, 0, :], ob[:, :]), (kT[:, 0, :], scores[:, 0:BANK]))):
                act.wait_ge(proj_ps, 2 * i + 1)
                act.activation(dst, src, ACT.Copy,
                               scale=SCALE if i == 0 else 1.0).then_inc(proj_act, 1)

            for m in range(PAIRS + 3):
                n, o, x, r = m, m - 1, m - 2, m - 3
                if 0 <= r:
                    act.wait_ge(rmax_ready, r + 1)
                    act.activation(pr[:, r, :], logit_cols, ACT.Exp, bias=rt[:, r, 0:1],
                                   accum_out=rt[:, r, 1:2]).then_inc(rexp_done, 1)
                if n < PAIRS:
                    act.wait_ge(negmax_ready, n + 1)
                    if n >= 1:
                        act.wait_ge(pt_ps, 4 * n)
                    for j in range(SB):
                        act.activation(probs[:, j * SC:(j + 1) * SC], score_bank(j), ACT.Exp, bias=nm[:, n:n + 1],
                                       accum_out=rs[:, 4 * n + j:4 * n + j + 1]).then_inc(exp_done, 1)
                    act.activation(probs[:, KV:KV + P], tails[:, :], ACT.Exp, bias=nm[:, n:n + 1],
                                   accum_out=rs[:, 4 * n + 3:4 * n + 4]).then_inc(exp_done, 1)
                    if n == 0:
                        act.wait_ge(proj_ps, 5)
                        act.copy(vn[:, 0:2, :], ob[:, :]).then_inc(proj_act, 1)
                if m == PAIRS:
                    for j in range(IC):
                        split_hi(0, j)
                if n < PAIRS:
                    for j in (0, 2):
                        act.wait_ge(pt_ps, 4 * n + j + 1)
                        if n >= 1 and j == 0:
                            act.wait_ge(pv_ps, n)
                        act.copy(probsT[0:CP, j * BANK:(j + 1) * BANK], ptb[0][0:CP, :]).then_inc(pt_act, 1)
                if 0 <= x < PAIRS:
                    act.wait_ge(x2T_ps, x + 1)
                    if x >= 1:
                        act.wait_ge(logit_ps, x)
                    act.copy(x2T[:, :, :], x2T_cols).then_inc(x2f_ready, 1)
                    act.copy(x2hi[:, :, x * PT:(x + 1) * PT].rearrange("p k (h s) -> p k h s", h=2),
                             halves(x2T_cols)).then_inc(x2hi_ready, 1)
                if 0 <= o < PAIRS:
                    act.wait_ge(oT_ps, o + 1)
                    if o >= 1:
                        act.wait_ge(wo_ps, o)
                    act.copy(oT[:, :], mb[:, 0:D]).then_inc(oT_ready, 1)

            def silu(u):
                act.wait_ge(gate_ready, u + 1)
                if u >= 2:
                    act.wait_ge(sw_done, u - 1)
                act.activation(sil[u % 2], gate_ps[u % 2], ACT.Silu).then_inc(silu_done, 1)

            silu(0)
            act.wait_ge(w16T_ps, 1)
            act.copy(w16T[:, :].rearrange("r (n h s) -> r n h s", n=PAIRS, h=2),
                     halves(mb[0:2 * E, :].rearrange("r (n t) -> r n t", n=PAIRS))).then_inc(w16T_ready, 1)
            silu(1)
            act.wait_ge(wb_ps_ready, 1)
            act.copy(wbs[0], wb_ps).then_inc(wb_ready, 1)

            for e in range(E):
                for j in range(IC):
                    u = IC * e + j
                    if u >= 2:
                        silu(u)
                    act.wait_ge(hid_done, u + 1)
                    if u >= 2:
                        act.wait_ge(down_done, u - 1)
                    act.copy(hhi[u % 2][:, :], hid[u % 2]).then_inc(hhi_done, 1)
                    if e + 1 < E:
                        split_hi(e + 1, j)
                        if j == 2:
                            act.wait_ge(wb_ps_ready, e + 2)
                            if e >= 1:
                                act.wait_ge(hid_done, IC * e)
                            act.copy(wbs[(e + 1) % 2], wb_ps).then_inc(wb_ready, 1)

            act.wait_ge(down_done, UNITS)
            act.copy(halves(xnT[:, 0, :].rearrange("p (n t) -> p n t", n=PAIRS)),
                     y_ps[0].rearrange("p (n h s) -> p n h s", n=PAIRS, h=2)).then_inc(yT_act, 1)
            out_v = out.rearrange("(n h) s d -> h s n d", h=2)
            for n in (0, 2):
                act.wait_ge(fin_ready, n + 2)
                act.dma_start(out_v[1, :, n:n + 2, :], fin[HALF:HALF + SQ, n:n + 2, :]).then_inc(out_done, 16)
            act.wait_ge(out_done, 16 * PAIRS)

        @block.vector
        def _(dve):
            steps = [0]

            def link(ins):
                steps[0] += 1
                ins.then_inc(dve_step, 1)
                dve.wait_ge(dve_step, steps[0])

            def layernorm(src, lo, hi, ready):
                for n in range(lo, hi):
                    ins = dve.bn_stats(stats[:, n, :], src[:, n, :])
                link(ins)
                for n in range(lo, hi):
                    ins = dve.bn_aggr(mv[:, n, :], stats[:, n, :])
                link(ins)
                z, s = nr[:, 3, lo:hi], nr[:, 4, lo:hi]
                link(dve.tensor_scalar(nr[:, 0, lo:hi], mv[:, lo:hi, 1], EPS, 64.0, ALU.add, ALU.mult))
                ins = dve.tensor_scalar(z.bitcast(I32), nr[:, 0, lo:hi].bitcast(I32), -0.5,
                                        float(0x5F3759DF - 2 ** 31), ALU.mult, ALU.add)
                dve.tensor_scalar(nr[:, 1, lo:hi], mv[:, lo:hi, 1], EPS, 16.0, ALU.add, ALU.mult)
                link(dve.tensor_scalar(nr[:, 2, lo:hi], mv[:, lo:hi, 1], EPS, 4.0, ALU.add, ALU.mult))
                for i in range(3):
                    v = nr[:, i, lo:hi]
                    if hi - lo == 1:
                        link(dve.scalar_tensor_tensor(s, z, v, z, ALU.mult, ALU.mult))
                    else:
                        link(dve.tensor_tensor(s, z, z, ALU.mult))
                        link(dve.tensor_tensor(s, s, v, ALU.mult))
                    link(dve.scalar_tensor_tensor(z, s, -3.0, z, ALU.add, ALU.mult))
                for n in range(lo, hi):
                    dve.tensor_scalar(xn[:, n, :], src[:, n, :], mv[:, n, 0:1], z[:, n - lo:n - lo + 1],
                                      ALU.subtract, ALU.mult).then_inc(ready, 1)

            dve.wait_ge(x_in, 16)
            layernorm(x0, 0, PAIRS, xn_ready)
            for h in range(2):
                c = slice(h * D, (h + 1) * D)
                dve.wait_ge(xnT_ps, 2 * h + 2)
                dve.tensor_copy(xnT[:, 1, c], xnT_banks[h][1][:, c]).then_inc(xnT_dve, 1)
            dve.wait_ge(proj_ps, 2)
            dve.tensor_scalar(qT[:, 1, :], mb[:, :], SCALE, None, ALU.mult).then_inc(proj_dve, 1)
            dve.wait_ge(proj_ps, 4)
            dve.tensor_copy(kT[:, 1, :], scores[:, BANK:2 * BANK]).then_inc(proj_dve, 1)
            dve.wait_ge(consts_ready, CONSTS)
            dve.tensor_copy(sel[:, :, :], self32).then_inc(sel_ready, 1)

            def router_max(r):
                dve.wait_ge(logit_ps, r + 1)
                dve.tensor_reduce(rt[:, r, 0:1], logit_cols, AXX, ALU.max, negate=True).then_inc(rmax_ready, 1)

            def router_weights(r):
                dve.wait_ge(rexp_done, r + 1)
                p, total = pr[:, r, :], rt[:, r, 1:2]
                pf = p.rearrange("q (a f) -> q a f", a=1).broadcast_to([P, E, E])
                pe = p.rearrange("q (f a) -> q f a", a=1).broadcast_to([P, E, E])
                dve.tensor_tensor(cmp[:, 0], pf, pe, ALU.is_gt)
                dve.tensor_tensor(cmp[:, 1], pf, pe, ALU.is_equal)
                dve.reciprocal(rt[:, r, 2:3], total)
                dve.tensor_scalar(rt[:, r, 3:4], total, TOP_P, None, ALU.mult)
                link(dve.tensor_tensor(cmp[:, 2], below[:, :, :], pf, ALU.mult))
                dve.tensor_tensor(before[:, :, 0, :], cmp[:, 0], pf, ALU.mult)
                dve.tensor_scalar(pn[:, :], p, rt[:, r, 2:3], None, ALU.mult)
                link(dve.tensor_tensor(before[:, :, 1, :], cmp[:, 1], cmp[:, 2], ALU.mult))
                link(dve.tensor_reduce(rex[:, :], before[:, :, :, :].rearrange("q e a f -> q e (a f)"), AXX, ALU.add))
                link(dve.scalar_tensor_tensor(rw8[:, :], rex[:, :], rt[:, r, 3:4], pn[:, :], ALU.is_le, ALU.mult))
                link(dve.tensor_copy(w16[:, r, 0:E], rw8[:, :]))
                dve.tensor_tensor(w16[:, r, E:2 * E], rw8[:, :], w16[:, r, 0:E].bitcast(F32),
                                  ALU.subtract).then_inc(w16_ready, 1)

            for m in range(PAIRS + 3):
                n, o, x, r = m, m - 1, m - 2, m - 3
                if n < PAIRS:
                    for j in range(SB):
                        dve.wait_ge(score_ps, SB * n + j + 1)
                        dve.tensor_reduce(mx[:, 4 * n + j:4 * n + j + 1], score_bank(j), AXX, ALU.max)
                if 0 <= r:
                    router_max(r)
                if n < PAIRS:
                    dve.wait_ge(tail_ps, n + 1)
                    if n >= 1:
                        dve.wait_ge(exp_done, 4 * n)
                    link(dve.tensor_tensor(tails[:, :], tail[:, 0:P], mask[:, :], ALU.add))
                    link(dve.tensor_reduce(mx[:, 4 * n + 3:4 * n + 4], tails[:, :], AXX, ALU.max))
                    dve.tensor_reduce(nm[:, n:n + 1], mx[:, 4 * n:4 * n + 4], AXX, ALU.max,
                                      negate=True).then_inc(negmax_ready, 1)
                    if n == 0:
                        dve.wait_ge(proj_ps, 6)
                        dve.tensor_copy(vn[:, 2:4, :], mb[:, :]).then_inc(proj_dve, 1)
                if 0 <= x < PAIRS:
                    dve.wait_ge(wo_ps, x + 1)
                    dve.tensor_tensor(x1[:, x, :], x0[:, x, :], mb[:, D:2 * D], ALU.add).then_inc(x1_ready, 1)
                    dve.wait_ge(x1_ready, x + 1)
                    layernorm(x1, x, x + 1, xn2_ready)
                if 0 <= r:
                    router_weights(r)
                if 0 <= o < PAIRS:
                    dve.wait_ge(exp_done, 4 * o + 4)
                    link(dve.tensor_reduce(rsum[:, o:o + 1], rs[:, 4 * o:4 * o + 4], AXX, ALU.add))
                    link(dve.reciprocal(rinv[:, o:o + 1], rsum[:, o:o + 1]))
                    dve.wait_ge(pv_ps, o + 1)
                    if o >= 1:
                        dve.wait_ge(oT_ps, o)
                    dve.tensor_scalar(on[:, :], ob[:, 0:D], rinv[:, o:o + 1], None, ALU.mult).then_inc(on_ready, 1)
                if n < PAIRS:
                    dve.wait_ge(pt_ps, 4 * n + 2)
                    if n >= 1:
                        dve.wait_ge(pv_ps, n)
                    dve.tensor_copy(probsT[0:CP, BANK:2 * BANK], ptb[1][0:CP, :]).then_inc(pt_dve, 1)
                    dve.wait_ge(pt_ps, 4 * n + 4)
                    dve.tensor_copy(probsT[:, CH * P:(CH + 1) * P], ptb[1][:, 0:P]).then_inc(pt_dve, 1)
                if 0 <= x < PAIRS:
                    dve.wait_ge(x2hi_ready, x + 1)
                    dve.tensor_tensor(x2lo[:, :, x * PT:(x + 1) * PT].rearrange("p k (h s) -> p k h s", h=2),
                                      halves(x2T_cols),
                                      x2hi[:, :, x * PT:(x + 1) * PT].bitcast(F32).rearrange("p k (h s) -> p k h s", h=2),
                                      ALU.subtract).then_inc(x2lo_ready, 1)

            for e in range(E):
                for j in range(IC):
                    u = IC * e + j
                    dve.wait_ge(silu_done, u + 1)
                    dve.wait_ge(up_ready, u + 1)
                    dve.tensor_tensor(sw[u % 2], sil[u % 2], up_ps[u % 2], ALU.mult).then_inc(sw_done, 1)
                    dve.wait_ge(sw_done, u + 1)
                    if j == 0:
                        dve.wait_ge(wb_ready, e + 1)
                    dve.tensor_tensor(hid[u % 2], sw[u % 2], wbs[e % 2], ALU.mult).then_inc(hid_done, 1)
                    dve.wait_ge(hhi_done, u + 1)
                    if u >= 2:
                        dve.wait_ge(down_done, u - 1)
                    dve.tensor_tensor(hlo[u % 2][:, :], hid[u % 2], hhi[u % 2][:, :].bitcast(F32),
                                      ALU.subtract).then_inc(hlo_done, 1)
                    if e + 1 < E:
                        dve.wait_ge(whi_done, IC * (e + 1) + j + 1)
                        c = PIECES[j]
                        dve.tensor_tensor(wlo[(e + 1) % 2][:, c], ring[(B + e + 1) % TSLOTS][:, c],
                                          whi[(e + 1) % 2][:, c].bitcast(F32), ALU.subtract).then_inc(wlo_done, 1)

            dve.wait_ge(down_done, UNITS)
            dve.tensor_copy(halves(xnT[:, 1, :].rearrange("p (n t) -> p n t", n=PAIRS)),
                            y_ps[1].rearrange("p (n h s) -> p n h s", n=PAIRS, h=2)).then_inc(yT_dve, 1)
            for n in range(PAIRS):
                src = (scores[:, n * BANK:n * BANK + D] if n < SB else tail[:, 0:D])
                dve.wait_ge(y_ps_ready, n + 1)
                dve.tensor_tensor(fin[:, n, :], x1[:, n, :], src, ALU.add).then_inc(fin_ready, 1)

        @block.tensor
        def _(pe):
            mm = nc.tensor.matmul

            def transpose(dst, src, last=None):
                ins = nc.tensor.transpose(dst, src, ident[0:src.shape[0], 0:src.shape[0]])
                if last is not None:
                    ins.then_inc(last, 1)

            pe.wait_ge(consts_ready, IDENT_STEPS)
            for h in range(2):
                pe.wait_ge(xn_ready, 2 * h + 2)
                for k in range(KD):
                    for n in (2 * h, 2 * h + 1):
                        transpose(xnT_banks[h][k][:, n * P:(n + 1) * P], xn[:, n, k * P:(k + 1) * P], xnT_ps if n % 2 else None)
            pe.wait_ge(wp_in, 16)
            for w, banks in ((0, (ob[:, :], mb[:, :])), (1, (scores[:, 0:BANK], scores[:, BANK:2 * BANK]))):
                for h in range(2):
                    c = slice(h * D, (h + 1) * D)
                    if w == 0:
                        pe.wait_ge(xnT_act, h + 1)
                        pe.wait_ge(xnT_dve, h + 1)
                    for m in range(KD):
                        for k in range(KD):
                            ins = mm(banks[m][:, c], wp[:, w, k, m * P:(m + 1) * P], xnT[:, k, c], start=k == 0,
                                     stop=k == KD - 1)
                        if h == 1:
                            ins.then_inc(proj_ps, 1)

            def project_values():
                for n in range(PAIRS):
                    if n == 0:
                        pe.wait_ge(proj_act, 1)
                    if n == 2:
                        pe.wait_ge(proj_dve, 1)
                    for k in range(KD):
                        ins = mm((ob if n < 2 else mb)[:, (n % 2) * D:(n % 2 + 1) * D], xnT[:, k, n * P:(n + 1) * P],
                                 wp[:, 2, k, :], start=k == 0, stop=k == KD - 1)
                    if n % 2:
                        ins.then_inc(proj_ps, 1)

            def logits(r):
                pe.wait_ge(x2f_ready, r + 1)
                pe.wait_ge(x2lo_ready, r + 1)
                if r == 0:
                    pe.wait_ge(rw_in, 16)
                for k in range(KD):
                    ins = mm(logit_cols, x2T[:, k, :], rws[:, k, :], start=k == 0, stop=k == KD - 1)
                ins.then_inc(logit_ps, 1)

            def split_ready(e, pieces):
                pe.wait_ge(whi_done, IC * e + pieces)
                pe.wait_ge(*((wlo0_done, pieces) if e == 0 else (wlo_done, IC * (e - 1) + pieces)))

            def gate_up(u, tokens=slice(0, TOK)):
                e, j = u // IC, u % IC
                g, up, _ = wcol(e, j)
                if j == 0:
                    split_ready(e, EARLY)
                for dst, cols, ready, freed in ((gate_ps, g, gate_ready, silu_done), (up_ps, up, up_ready, sw_done)):
                    if u >= 2:
                        pe.wait_ge(freed, u - 1)
                    n = 0
                    for k in range(KD):
                        for w, xx in ((whi, x2hi), (whi, x2lo), (wlo, x2hi)):
                            ins = mm(dst[u % 2][:, tokens], w[e % 2][:, cols[k]], xx[:, k, tokens], start=n == 0,
                                     stop=n == 3 * KD - 1)
                            n += 1
                    if tokens.stop == TOK:
                        ins.then_inc(ready, 1)

            def down(u):
                e, j = u // IC, u % IC
                _, _, d = wcol(e, j)
                if j == 1:
                    split_ready(e, IC)
                pe.wait_ge(hhi_done, u + 1)
                pe.wait_ge(hlo_done, u + 1)
                for m in range(KD):
                    for i, (w, h) in enumerate(((whi, hhi), (whi, hlo), (wlo, hhi))):
                        ins = mm(y_ps[m], w[e % 2][:, d[m]], h[u % 2][:, :], start=u == 0 and i == 0,
                                 stop=u == UNITS - 1 and i == 2)
                ins.then_inc(down_done, 1)

            def weight_rows(e):
                if e >= 1:
                    pe.wait_ge(wb_ready, e)
                mm(wb_ps, sel[:, e, :], w16T[:, :], start=True, stop=True).then_inc(wb_ps_ready, 1)

            for m in range(PAIRS + 3):
                n, o, x, r = m, m - 1, m - 2, m - 3
                if n < PAIRS:
                    if n == 0:
                        pe.wait_ge(proj_act, 2)
                        pe.wait_ge(proj_dve, 2)
                    else:
                        pe.wait_ge(exp_done, 4 * n - 1)
                    ring_arrived(pe, 2 * n)
                    ring_arrived(pe, 2 * n + 1)
                    for j in range(SB):
                        for k in range(KD):
                            for h in range(2):
                                ins = mm(scores[h * HALF:(h + 1) * HALF, j * BANK:j * BANK + SC],
                                         qT[:, k, n * P + h * HALF:n * P + (h + 1) * HALF],
                                         ring[(2 * n + h) % TSLOTS][:, k * KV + j * SC:k * KV + (j + 1) * SC],
                                         start=k == 0, stop=k == KD - 1, tile_position=(0, h * HALF))
                        ins.then_inc(score_ps, 1)
                if 0 <= r:
                    logits(r)
                if 0 <= x < PAIRS:
                    pe.wait_ge(oT_ready, x + 1)
                    for k in range(KD):
                        ins = mm(mb[:, D:2 * D], oT[:, k * P:(k + 1) * P], wp[:, 3, k, :], start=k == 0, stop=k == KD - 1)
                    ins.then_inc(wo_ps, 1)
                if x == PAIRS - 1:
                    gate_up(0, slice(0, HT))
                if n < PAIRS:
                    if 0 <= x:
                        pe.wait_ge(x2lo_ready, x)
                    if 0 <= r:
                        pe.wait_ge(rexp_done, r + 1)
                    for k in range(KD):
                        ins = mm(tail[:, 0:P], qT[:, k, n * P:(n + 1) * P], kT[:, k, n * P:(n + 1) * P],
                                 start=k == 0, stop=k == KD - 1)
                    ins.then_inc(tail_ps, 1)
                    if n == 0:
                        project_values()
                if 0 <= o < PAIRS:
                    if o == 0:
                        pe.wait_ge(proj_act, 3)
                    else:
                        pe.wait_ge(on_ready, o)
                    for c in range(CH):
                        j = c // GC
                        if c % GC == 0:
                            if j % 2:
                                pe.wait_ge(pt_dve, 2 * o + 1)
                            else:
                                pe.wait_ge(pt_act, 2 * o + j // 2 + 1)
                        if c == 0:
                            rows_arrived(pe, 2 * o)
                            rows_arrived(pe, 2 * o + 1)
                        for h in range(2):
                            mm(ob[h * HALF:(h + 1) * HALF, 0:D], probsT[0:CP, c * P + h * HALF:c * P + (h + 1) * HALF],
                               rows[(2 * o + h) % NSLOTS][0:CP, c * D:(c + 1) * D], start=c == 0, stop=False,
                               tile_position=(0, h * HALF), skip_group_check=True)
                    pe.wait_ge(pt_dve, 2 * o + 2)
                    if o == 0:
                        pe.wait_ge(proj_dve, 3)
                    mm(ob[:, 0:D], probsT[:, CH * P:(CH + 1) * P], vn[:, o, :], start=False, stop=True,
                       skip_group_check=True).then_inc(pv_ps, 1)
                if n < PAIRS:
                    for j in range(SB + 1):
                        g = 4 * n + j
                        pe.wait_ge(exp_done, g + 1)
                        if g >= 2:
                            pe.wait_ge(pt_dve if j % 2 else pt_act, g // 2)
                        if j < SB:
                            for i in range(GC):
                                c = GC * j + i
                                transpose(ptb[j % 2][0:CP, i * P:(i + 1) * P], probs[:, c * CP:(c + 1) * CP],
                                          pt_ps if i == GC - 1 else None)
                        else:
                            transpose(ptb[j % 2][:, 0:P], probs[:, KV:KV + P], pt_ps)
                if 0 <= x < PAIRS:
                    pe.wait_ge(xn2_ready, x + 1)
                    if x >= 1:
                        pe.wait_ge(rexp_done, x)
                    for k in range(KD):
                        transpose(x2T_cols[:, k, :], xn[:, x, k * P:(k + 1) * P], x2T_ps if k == KD - 1 else None)
                    if x == PAIRS - 1:
                        gate_up(1, slice(0, HT))
                if 0 <= o < PAIRS:
                    pe.wait_ge(on_ready, o + 1)
                    if o == 0:
                        pe.wait_ge(proj_dve, 3)
                    else:
                        pe.wait_ge(x1_ready, o)
                    for k in range(KD):
                        transpose(mb[:, k * P:(k + 1) * P], on[:, k * P:(k + 1) * P], oT_ps if k == KD - 1 else None)

            gate_up(0, slice(HT, TOK))
            pe.wait_ge(w16_ready, PAIRS)
            for n in range(PAIRS):
                transpose(mb[0:2 * E, n * P:(n + 1) * P], w16[:, n, :].bitcast(F32), w16T_ps if n == PAIRS - 1 else None)
            gate_up(1, slice(HT, TOK))
            pe.wait_ge(w16T_ready, 1)
            pe.wait_ge(sel_ready, 1)
            pe.wait_ge(rexp_done, PAIRS)
            weight_rows(0)
            gate_up(2)
            down(0)
            for u in range(2, UNITS):
                if u > 2:
                    gate_up(u)
                down(u - 1)
                if u % IC == 2 and u // IC + 1 < E:
                    weight_rows(u // IC + 1)
            down(UNITS - 1)

            pe.wait_ge(yT_act, 1)
            pe.wait_ge(yT_dve, 1)
            for n in range(PAIRS):
                dst = scores[:, n * BANK:n * BANK + D] if n < SB else tail[:, 0:D]
                for k in range(KD):
                    transpose(dst[:, k * P:(k + 1) * P], xnT[:, k, n * P:(n + 1) * P], y_ps_ready if k == KD - 1 else None)


def kernel(x, ctx_2048, mask_BxSx4224_bf0, L0_xattn_wq, L0_xattn_wk, L0_xattn_wv, L0_xattn_wo,
           L0_ffn_router_w, L0_ffn_gate_w, L0_ffn_up_w, L0_ffn_down_w):
    import concourse.bacc as bacc
    from concourse.bass_utils import run_bass_kernel_spmd

    x = np.asarray(x)
    ctx = np.asarray(ctx_2048)
    xp = np.zeros((2, HALF, PAIRS, D), x.dtype)
    xp[:, :SQ] = x.reshape(PAIRS, 2, SQ, D).transpose(1, 2, 0, 3)
    proj = np.stack([np.asarray(w).T.reshape(KD, P, D).transpose(1, 0, 2)
                     for w in (L0_xattn_wq, L0_xattn_wk, L0_xattn_wv, L0_xattn_wo)], axis=1)
    router = np.asarray(L0_ffn_router_w).T.reshape(KD, P, E).transpose(1, 0, 2)
    ctx_t = ctx.reshape(B, CP, CH, KD, P).transpose(0, 4, 3, 2, 1).reshape(B, P, KD * KV)
    ctx_n = np.zeros((B, P, CH * D), ctx.dtype)
    ctx_n[:, :CP] = ctx.reshape(B, CP, CH * D)

    def width_first(w):
        return np.asarray(w).transpose(0, 2, 1).reshape(E, KD, P, I).transpose(0, 2, 1, 3).reshape(E, P, GW)

    down = np.asarray(L0_ffn_down_w).transpose(0, 2, 1).reshape(E, IC, P, D).transpose(0, 2, 1, 3).reshape(E, P, IC * D)
    wffn = np.concatenate([width_first(L0_ffn_gate_w), width_first(L0_ffn_up_w), down], axis=2)

    arrays = {"xp": xp.reshape(P, PAIRS, D), "wproj": proj, "router": router,
              "ctx_t": ctx_t, "ctx_n": ctx_n, "wffn": wffn}
    arrays = {k: np.ascontiguousarray(v) for k, v in arrays.items()}
    nc = bacc.Bacc("TRN2", target_bir_lowering=False, num_devices=1)
    args = [nc.dram_tensor(k, v.shape, mybir.dt.from_np(v.dtype), kind="ExternalInput").ap() for k, v in arrays.items()]
    args.append(nc.dram_tensor("out", (B, SQ, D), F32, kind="ExternalOutput").ap())
    build(nc, *args)
    result = run_bass_kernel_spmd(nc, [arrays], core_ids=[0])
    return result.results[0]["out"]
```

```python
from contextlib import ExitStack

import numpy as np

import concourse.bass as bass
from concourse import mybir

F32 = mybir.dt.float32
F32R = mybir.dt.float32r
I32 = mybir.dt.int32
ALU = mybir.AluOpType
ACT = mybir.ActivationFunctionType
AXX = mybir.AxisListType.X

P = 128
B, SQ, D = 8, 56, 256
KV = 1500
E, I = 8, 512
HALF = P // 2
PAIRS = B // 2
KD = D // P
CH = 12
CP = KV // CH
SB = 3
SC = KV // SB
GC = CH // SB
BANK = 512
TOK = B * SQ
PT = 2 * SQ
IC = I // P
UNITS = E * IC
CCOLS = (2 * KD + KD) * P
WCOLS = IC * CCOLS
TSLOTS, NSLOTS = 3, 4
LO_DVE = 2 * IC
HT = TOK // 2
SCALE = 1.0 / 16.0
EPS = 1e-5
TOP_P = 0.9
MASKED = -3.0e38
WARM = 22
IDENT_STEPS, CONSTS = 2, 10


def build(nc, x, wproj, rw, ctx_t, ctx_n, wffn, out):
    with ExitStack() as ctx:
        def sb(name, shape, dt=F32):
            return ctx.enter_context(nc.sbuf_tensor(name, shape, dt))

        def pb(name, cols):
            return ctx.enter_context(nc.psum_tensor(name, [P, cols], F32))

        def sem(name):
            return ctx.enter_context(nc.semaphore(name))

        scores = pb("scores", SB * BANK)
        tail = pb("tail", BANK)
        ptb = [pb(f"ptb{i}", BANK) for i in range(2)]
        ob = pb("ob", BANK)
        mb = pb("mb", BANK)
        gate_ps = [scores[:, 0:TOK], scores[:, 2 * BANK:2 * BANK + TOK]]
        up_ps = [scores[:, BANK:BANK + TOK], ob[:, 0:TOK]]
        y_ps = [ptb[0][:, 0:TOK], ptb[1][:, 0:TOK]]
        gate_bank = [ptb[0][:, 0:TOK] if u == 2 else gate_ps[u % 2] for u in range(UNITS)]
        up_bank = [ptb[1][:, 0:TOK] if u == 2 else up_ps[u % 2] for u in range(UNITS)]
        wb_ps = tail[:, 0:TOK]
        pt_banks = [ptb[0][:, :], ptb[1][:, :], scores[:, 2 * BANK:3 * BANK], scores[:, BANK:2 * BANK]]
        x2T_cols = tail[:, P:3 * P].rearrange("p (k t) -> p k t", k=KD)
        xnT_banks = [ptb, [scores[:, 2 * BANK:3 * BANK], tail]]
        q_banks = [[ob, mb], ptb]
        k_banks = [ob, mb]
        v_banks = ptb
        logit_cols = tail[:, 3 * P:3 * P + E]

        ring = [sb(f"ring{i}", [P, WCOLS]) for i in range(TSLOTS)]
        rows = [sb(f"rows{i}", [P, CH * D]) for i in range(NSLOTS)]
        whi = [sb(f"whi{i}", [P, WCOLS], F32R) for i in range(2)]
        wlo = [sb(f"wlo{i}", [P, WCOLS], F32R) for i in range(2)]
        x0 = sb("x0", [P, PAIRS, D])
        x1 = sb("x1", [P, PAIRS, D])
        xn = sb("xn", [P, PAIRS, D])
        xnT = sb("xnT", [P, KD, PAIRS * P])
        qT = sb("qT", [P, KD, PAIRS * P])
        kT = sb("kT", [P, KD, PAIRS * P])
        vn = sb("vn", [P, PAIRS, D])
        wp = sb("wp", [P, 4, KD, D])
        rws = sb("rws", [P, KD, E])
        probs = sb("probs", [P, KV + P])
        probsT = sb("probsT", [P, (CH + 1) * P])
        tails = sb("tails", [P, P])
        on = sb("on", [P, D])
        oT = sb("oT", [P, D])
        x2T = sb("x2T", [P, KD, P])
        x2hi = sb("x2hi", [P, KD, TOK], F32R)
        x2lo = sb("x2lo", [P, KD, TOK], F32R)
        hhi = [sb(f"hhi{i}", [P, TOK], F32R) for i in range(2)]
        hlo = [sb(f"hlo{i}", [P, TOK], F32R) for i in range(2)]
        ident = sb("ident", [P, P])
        mask = sb("mask", [P, P])
        below = sb("below", [P, E, E])
        self32 = x1[0:2 * E, :, :].rearrange("r n d -> r (n d)").rearrange("r (e m) -> r e m", e=E)
        sel = sb("sel", [2 * E, E, P], F32R)
        w16 = sb("w16", [P, PAIRS, 2 * E], F32R)
        w16T = sb("w16T", [2 * E, TOK], F32R)
        stats = sb("stats", [P, PAIRS, 6])
        mv = sb("mv", [P, PAIRS, 2])
        nr = sb("nr", [P, 5, PAIRS])
        mx = sb("mx", [P, 4 * PAIRS])
        nm = sb("nm", [P, PAIRS])
        rs = sb("rs", [P, 4 * PAIRS])
        rsum = sb("rsum", [P, PAIRS])
        rinv = sb("rinv", [P, PAIRS])
        rt = sb("rt", [P, PAIRS, 8])
        pr = sb("pr", [P, PAIRS, E])
        rex = sb("rex", [P, E])
        sil = [rows[0][:, i * BANK:i * BANK + TOK] for i in range(2)]
        sw = [rows[0][:, (2 + i) * BANK:(2 + i) * BANK + TOK] for i in range(2)]
        hid = [rows[0][:, (4 + i) * BANK:(4 + i) * BANK + TOK] for i in range(2)]
        wbs = [rows[1][:, i * BANK:i * BANK + TOK] for i in range(2)]
        fin = rows[1][:, 2 * BANK:2 * BANK + PAIRS * D].rearrange("p (n d) -> p n d", n=PAIRS)
        cmp = sb("cmp", [P, 3, E, E])
        before = sb("before", [P, E, 2, E])
        pn = sb("pn", [P, E])
        rw8 = sb("rw8", [P, E])

        x_in, wp_in, wo_in, rw_in = sem("x_in"), sem("wp_in"), sem("wo_in"), sem("rw_in")
        ring_in = [[sem(f"ring_in{i}_{part}") for part in range(2)] for i in range(TSLOTS)]
        rows_in = [[sem(f"rows_in{i}_{part}") for part in range(SB)] for i in range(NSLOTS)]
        consts_ready, sel_ready = sem("consts_ready"), sem("sel_ready")
        dve_step = sem("dve_step")
        xn_ready, xnT_ps, xnT_act, xnT_dve = sem("xn_ready"), sem("xnT_ps"), sem("xnT_act"), sem("xnT_dve")
        q_ps, q_act, q_dve = sem("q_ps"), sem("q_act"), sem("q_dve")
        k_ps, k_act, k_dve = sem("k_ps"), sem("k_act"), sem("k_dve")
        v_ps, v_act, v_dve = sem("v_ps"), sem("v_act"), sem("v_dve")
        score_ps, tail_ps, negmax_ready, exp_done = sem("score_ps"), sem("tail_ps"), sem("negmax_ready"), sem("exp_done")
        pt_ps, pt_act, pt_dve, pv_ps = sem("pt_ps"), sem("pt_act"), sem("pt_dve"), sem("pv_ps")
        on_ready, oT_ps, oT_ready, wo_ps = sem("on_ready"), sem("oT_ps"), sem("oT_ready"), sem("wo_ps")
        x1_ready, xn2_ready, x2T_ps = sem("x1_ready"), sem("xn2_ready"), sem("x2T_ps")
        x2f_ready, x2hi_ready, x2lo_ready = sem("x2f_ready"), sem("x2hi_ready"), sem("x2lo_ready")
        logit_ps, rmax_ready, rexp_done, w16_ready = sem("logit_ps"), sem("rmax_ready"), sem("rexp_done"), sem("w16_ready")
        w16T_ps, w16T_ready, wb_ps_ready, wb_ready = sem("w16T_ps"), sem("w16T_ready"), sem("wb_ps_ready"), sem("wb_ready")
        gate_ready, up_ready, silu_done = sem("gate_ready"), sem("up_ready"), sem("silu_done")
        sw_done, hid_done, hhi_done, hlo_done = sem("sw_done"), sem("hid_done"), sem("hhi_done"), sem("hlo_done")
        whi_done, wlo_pool, wlo_done, down_done = sem("whi_done"), sem("wlo_pool"), sem("wlo_done"), sem("down_done")
        yT_act, yT_dve, y_ps_ready, fin_ready = sem("yT_act"), sem("yT_dve"), sem("y_ps_ready"), sem("fin_ready")
        out_done = sem("out_done")

        block = ctx.enter_context(nc.Block())

        def score_bank(j):
            return scores[:, j * BANK:j * BANK + SC]

        def ring_parts(item):
            if item < B:
                return slice(0, KD * SC), slice(KD * SC, KD * KV)
            return slice(0, WCOLS // 2), slice(WCOLS // 2, WCOLS)

        def ring_arrived(eng, item, part):
            eng.wait_ge(ring_in[item % TSLOTS][part], 16 * (item // TSLOTS + 1))

        def weights_arrived(eng, u):
            ring_arrived(eng, B + u // IC, u % IC // (IC // 2))

        def lo_split(eng, u):
            eng.wait_ge(*((wlo_pool, u + 1) if u < LO_DVE else (wlo_done, u + 1 - LO_DVE)))

        def token_parts(u):
            return [slice(0, HT), slice(HT, TOK)] if u == UNITS - 1 else [slice(0, TOK)]

        def chunk_cols(u):
            return slice(u % IC * CCOLS, (u % IC + 1) * CCOLS)

        def packed(u):
            return ring[(B + u // IC) % TSLOTS][:, chunk_cols(u)]

        def rows_arrived(eng, b, part):
            eng.wait_ge(rows_in[b % NSLOTS][part], 16 * (b // NSLOTS + 1))

        def halves(ap):
            return ap.rearrange("p k (h s) -> p k h s", h=2)[:, :, :, 0:SQ]

        def tiles(w, u):
            t = [w[u // IC % 2][:, u % IC * CCOLS + i * P:u % IC * CCOLS + (i + 1) * P] for i in range(3 * KD)]
            return t[0:KD], t[KD:2 * KD], t[2 * KD:3 * KD]

        @block.sync
        def _(sp):
            sp.dma_start(x0[:, :, :], x).then_inc(x_in, 16)
            sp.dma_start(wp[:, 0:3, :, :], wproj[:, 0:3]).then_inc(wp_in, 16)

            def load_ring(item, src, part):
                c = ring_parts(item)[part]
                sp.dma_start(ring[item % TSLOTS][:, c], src[:, c]).then_inc(ring_in[item % TSLOTS][part], 16)

            def load_columns(b, part):
                if b >= TSLOTS:
                    sp.wait_ge(score_ps, SB * ((b - TSLOTS) // 2 + 1))
                load_ring(b, ctx_t[b], part)

            def load_rows(b, part):
                if b >= NSLOTS:
                    sp.wait_ge(pv_ps, (b - NSLOTS) // 2 + 1)
                c = slice(part * GC * D, (part + 1) * GC * D)
                sp.dma_start(rows[b % NSLOTS][:, c], ctx_n[b, :, c]).then_inc(rows_in[b % NSLOTS][part], 16)

            def load_expert(e):
                item = B + e
                if e < TSLOTS:
                    sp.wait_ge(score_ps, SB * ((item - TSLOTS) // 2 + 1))
                else:
                    sp.wait_ge(whi_done, IC * (e - TSLOTS + 1))
                    lo_split(sp, IC * (e - TSLOTS + 1) - 1)
                for part in range(2):
                    load_ring(item, wffn[e], part)

            for part in range(2):
                for b in (0, 1):
                    load_columns(b, part)
            for part in range(2):
                load_columns(2, part)
            load_rows(0, 0)
            load_rows(1, 0)
            load_rows(0, 1)
            for part in range(2):
                load_columns(3, part)
            sp.dma_start(wp[:, 3, :, :], wproj[:, 3]).then_inc(wo_in, 16)
            sp.dma_start(rws[:, :, :], rw).then_inc(rw_in, 16)
            for b, part in ((1, 1), (0, 2), (1, 2)):
                load_rows(b, part)
            for b in (4, 5):
                for part in range(2):
                    load_columns(b, part)
            for part in range(SB):
                for b in (2, 3):
                    load_rows(b, part)
            for part in range(2):
                for b in (6, 7):
                    load_columns(b, part)
            for pair in (2, 3):
                for part in range(SB):
                    for b in (2 * pair, 2 * pair + 1):
                        load_rows(b, part)
            for e in range(E):
                load_expert(e)
            out_v = out.rearrange("(n h) s d -> h s n d", h=2)
            for n in (0, 2):
                sp.wait_ge(fin_ready, n + 2)
                sp.dma_start(out_v[0, :, n:n + 2, :], fin[0:SQ, n:n + 2, :]).then_inc(out_done, 16)
            sp.wait_ge(out_done, 16 * PAIRS)

        @block.gpsimd
        def _(pool):
            built = [0]

            def made(ins):
                built[0] += 1
                ins.then_inc(consts_ready, 1)
                pool.wait_ge(consts_ready, built[0])

            made(pool.memset(ident[:, :], 0.0))
            made(pool.affine_select(out=ident[:, :], in_=ident[:, :], compare_op=ALU.not_equal, fill=1.0, base=0,
                                    pattern=[[-1, P]], channel_multiplier=1))
            made(pool.memset(mask[:, :], MASKED))
            made(pool.memset(mask[0:HALF, 0:SQ], 0.0))
            made(pool.memset(mask[HALF:P, HALF:HALF + SQ], 0.0))
            made(pool.memset(below[:, :, :], 0.0))
            made(pool.affine_select(out=below[:, :, :], in_=below[:, :, :], compare_op=ALU.is_ge, fill=1.0, base=0,
                                    pattern=[[-1, E], [1, E]], channel_multiplier=0))
            made(pool.memset(self32, 0.0))
            for part in range(2):
                made(pool.affine_select(out=self32, in_=self32, compare_op=ALU.not_equal, fill=1.0, base=-part * E,
                                        pattern=[[-1, E], [0, P]], channel_multiplier=1))
            assert built[0] == CONSTS
            for u in range(LO_DVE):
                weights_arrived(pool, u)
                pool.wait_ge(whi_done, u + 1)
                pool.tensor_tensor(wlo[u // IC][:, chunk_cols(u)], packed(u), whi[u // IC][:, chunk_cols(u)].bitcast(F32),
                                   ALU.subtract).then_inc(wlo_pool, 1)
                pool.wait_ge(wlo_pool, u + 1)

        @block.scalar
        def _(act):
            def split_hi(u):
                weights_arrived(act, u)
                if u >= 2 * IC:
                    act.wait_ge(down_done, u - 2 * IC + 1)
                act.copy(whi[u // IC % 2][:, chunk_cols(u)], packed(u)).then_inc(whi_done, 1)

            def q_to_sbuf(h):
                act.wait_ge(q_ps, 2 * h + 1)
                c = slice(h * D, (h + 1) * D)
                act.activation(qT[:, 0, c], q_banks[h][0][:, c], ACT.Copy, scale=SCALE).then_inc(q_act, 1)

            for h in range(2):
                c = slice(h * D, (h + 1) * D)
                act.wait_ge(xnT_ps, 2 * h + 1)
                act.copy(xnT[:, 0, c], xnT_banks[h][0][:, c]).then_inc(xnT_act, 1)
            q_to_sbuf(0)
            q_to_sbuf(1)
            act.wait_ge(k_ps, 1)
            act.copy(kT[:, 0, :], k_banks[0][:, :]).then_inc(k_act, 1)
            act.wait_ge(v_ps, 1)
            act.copy(vn[:, 0:2, :], v_banks[0][:, :]).then_inc(v_act, 1)

            for m in range(PAIRS + 3):
                n, o, x, r = m, m - 1, m - 2, m - 3
                if 0 <= r:
                    act.wait_ge(rmax_ready, r + 1)
                    act.activation(pr[:, r, :], logit_cols, ACT.Exp, bias=rt[:, r, 0:1],
                                   accum_out=rt[:, r, 1:2]).then_inc(rexp_done, 1)
                if n < PAIRS:
                    act.wait_ge(negmax_ready, n + 1)
                    if n >= 1:
                        act.wait_ge(pt_ps, 4 * n)
                    for j in range(SB):
                        act.activation(probs[:, j * SC:(j + 1) * SC], score_bank(j), ACT.Exp, bias=nm[:, n:n + 1],
                                       accum_out=rs[:, 4 * n + j:4 * n + j + 1]).then_inc(exp_done, 1)
                    act.activation(probs[:, KV:KV + P], tails[:, :], ACT.Exp, bias=nm[:, n:n + 1],
                                   accum_out=rs[:, 4 * n + 3:4 * n + 4]).then_inc(exp_done, 1)
                if m == PAIRS:
                    split_hi(0)
                    split_hi(1)
                if m == PAIRS + 1:
                    for u in range(IC, 2 * IC - 1):
                        split_hi(u)
                if m == PAIRS + 2:
                    split_hi(2 * IC - 1)
                if n < PAIRS:
                    for j in (0, 2):
                        act.wait_ge(pt_ps, 4 * n + j + 1)
                        if n >= 1 and j == 0:
                            act.wait_ge(pv_ps, n)
                        act.copy(probsT[0:CP, j * BANK:(j + 1) * BANK], pt_banks[j][0:CP, :]).then_inc(pt_act, 1)
                if 0 <= x < PAIRS:
                    act.wait_ge(x2T_ps, x + 1)
                    if x >= 1:
                        act.wait_ge(logit_ps, x)
                    act.copy(x2T[:, :, :], x2T_cols).then_inc(x2f_ready, 1)
                    act.copy(x2hi[:, :, x * PT:(x + 1) * PT].rearrange("p k (h s) -> p k h s", h=2),
                             halves(x2T_cols)).then_inc(x2hi_ready, 1)
                if 0 <= o < PAIRS:
                    act.wait_ge(oT_ps, o + 1)
                    if o >= 1:
                        act.wait_ge(wo_ps, o)
                    act.copy(oT[:, :], mb[:, 0:D]).then_inc(oT_ready, 1)
                if m == PAIRS:
                    split_hi(2)
                    split_hi(3)

            def silu(u):
                act.wait_ge(gate_ready, u + 1)
                if u >= 2:
                    act.wait_ge(sw_done, u - 1)
                act.activation(sil[u % 2], gate_bank[u], ACT.Silu).then_inc(silu_done, 1)

            def hidden_hi(u):
                for i, t in enumerate(token_parts(u)):
                    act.wait_ge(hid_done, u + 1 + i)
                    if u >= 2:
                        act.wait_ge(down_done, u - 1)
                    act.copy(hhi[u % 2][:, t], hid[u % 2][:, t]).then_inc(hhi_done, 1)

            def weights_to_sbuf(e):
                act.wait_ge(wb_ps_ready, e + 1)
                if e >= 2:
                    act.wait_ge(hid_done, IC * (e - 1))
                act.copy(wbs[e % 2], wb_ps).then_inc(wb_ready, 1)

            silu(0)
            silu(1)
            act.wait_ge(w16T_ps, 1)
            act.copy(w16T[:, :].rearrange("r (n h s) -> r n h s", n=PAIRS, h=2),
                     halves(mb[0:2 * E, :].rearrange("r (n t) -> r n t", n=PAIRS))).then_inc(w16T_ready, 1)
            weights_to_sbuf(0)
            hidden_hi(0)
            silu(2)
            hidden_hi(1)
            silu(3)
            hidden_hi(2)
            weights_to_sbuf(1)
            hidden_hi(3)
            split_hi(2 * IC)
            for u in range(IC, UNITS):
                silu(u)
                hidden_hi(u)
                if u + IC + 1 < UNITS:
                    split_hi(u + IC + 1)
                if u % IC == 2 and u // IC + 1 < E:
                    weights_to_sbuf(u // IC + 1)

            act.wait_ge(down_done, UNITS)
            for h in range(2):
                c, t = slice(h * D, (h + 1) * D), slice(h * HT, (h + 1) * HT)
                act.copy(halves(xnT[:, 0, c].rearrange("p (n t) -> p n t", n=2)),
                         y_ps[0][:, t].rearrange("p (n h s) -> p n h s", n=2, h=2)).then_inc(yT_act, 1)
            out_v = out.rearrange("(n h) s d -> h s n d", h=2)
            for n in (0, 2):
                act.wait_ge(fin_ready, n + 2)
                act.dma_start(out_v[1, :, n:n + 2, :], fin[HALF:HALF + SQ, n:n + 2, :]).then_inc(out_done, 16)
            act.wait_ge(out_done, 16 * PAIRS)

        @block.vector
        def _(dve):
            steps = [0]

            def link(ins):
                steps[0] += 1
                ins.then_inc(dve_step, 1)
                dve.wait_ge(dve_step, steps[0])

            def layernorm(src, lo, hi, ready):
                for n in range(lo, hi):
                    ins = dve.bn_stats(stats[:, n, :], src[:, n, :])
                link(ins)
                for n in range(lo, hi):
                    ins = dve.bn_aggr(mv[:, n, :], stats[:, n, :])
                link(ins)
                z, s = nr[:, 3, lo:hi], nr[:, 4, lo:hi]
                link(dve.tensor_scalar(nr[:, 0, lo:hi], mv[:, lo:hi, 1], EPS, 256.0 / 9.0, ALU.add, ALU.mult))
                dve.tensor_scalar(nr[:, 1, lo:hi], mv[:, lo:hi, 1], EPS, 64.0 / 9.0, ALU.add, ALU.mult)
                link(dve.tensor_scalar(z.bitcast(I32), nr[:, 0, lo:hi].bitcast(I32), -0.5,
                                       float(0x5F3759DF - 2 ** 31), ALU.mult, ALU.add))

                def squared(v):
                    if hi - lo == 1:
                        link(dve.scalar_tensor_tensor(s, z, v, z, ALU.mult, ALU.mult))
                    else:
                        link(dve.tensor_tensor(s, z, z, ALU.mult))
                        link(dve.tensor_tensor(s, s, v, ALU.mult))

                squared(nr[:, 0, lo:hi])
                link(dve.scalar_tensor_tensor(z, s, -3.0, z, ALU.add, ALU.mult))
                squared(nr[:, 1, lo:hi])
                link(dve.scalar_tensor_tensor(nr[:, 2, lo:hi], s, -10.0 / 3.0, s, ALU.add, ALU.mult))
                link(dve.scalar_tensor_tensor(z, nr[:, 2, lo:hi], 5.0, z, ALU.add, ALU.mult))
                for n in range(lo, hi):
                    dve.tensor_scalar(xn[:, n, :], src[:, n, :], mv[:, n, 0:1], z[:, n - lo:n - lo + 1],
                                      ALU.subtract, ALU.mult).then_inc(ready, 1)

            def q_to_sbuf(h):
                dve.wait_ge(q_ps, 2 * h + 2)
                c = slice(h * D, (h + 1) * D)
                dve.tensor_scalar(qT[:, 1, c], q_banks[h][1][:, c], SCALE, None, ALU.mult).then_inc(q_dve, 1)

            dve.wait_ge(x_in, 16)
            layernorm(x0, 0, PAIRS, xn_ready)
            for h in range(2):
                c = slice(h * D, (h + 1) * D)
                dve.wait_ge(xnT_ps, 2 * h + 2)
                dve.tensor_copy(xnT[:, 1, c], xnT_banks[h][1][:, c]).then_inc(xnT_dve, 1)
            q_to_sbuf(0)
            q_to_sbuf(1)
            dve.wait_ge(consts_ready, CONSTS)
            dve.tensor_copy(sel[:, :, :], self32).then_inc(sel_ready, 1)

            def router_max(r):
                dve.wait_ge(logit_ps, r + 1)
                dve.tensor_reduce(rt[:, r, 0:1], logit_cols, AXX, ALU.max, negate=True).then_inc(rmax_ready, 1)

            def router_weights(r):
                dve.wait_ge(rexp_done, r + 1)
                p, total = pr[:, r, :], rt[:, r, 1:2]
                pf = p.rearrange("q (a f) -> q a f", a=1).broadcast_to([P, E, E])
                pe = p.rearrange("q (f a) -> q f a", a=1).broadcast_to([P, E, E])
                dve.tensor_tensor(cmp[:, 0], pf, pe, ALU.is_gt)
                dve.tensor_tensor(cmp[:, 1], pf, pe, ALU.is_equal)
                dve.reciprocal(rt[:, r, 2:3], total)
                dve.tensor_scalar(rt[:, r, 3:4], total, TOP_P, None, ALU.mult)
                link(dve.tensor_tensor(cmp[:, 2], below[:, :, :], pf, ALU.mult))
                dve.tensor_tensor(before[:, :, 0, :], cmp[:, 0], pf, ALU.mult)
                dve.tensor_scalar(pn[:, :], p, rt[:, r, 2:3], None, ALU.mult)
                link(dve.tensor_tensor(before[:, :, 1, :], cmp[:, 1], cmp[:, 2], ALU.mult))
                link(dve.tensor_reduce(rex[:, :], before[:, :, :, :].rearrange("q e a f -> q e (a f)"), AXX, ALU.add))
                link(dve.scalar_tensor_tensor(rw8[:, :], rex[:, :], rt[:, r, 3:4], pn[:, :], ALU.is_le, ALU.mult))
                link(dve.tensor_copy(w16[:, r, 0:E], rw8[:, :]))
                dve.tensor_tensor(w16[:, r, E:2 * E], rw8[:, :], w16[:, r, 0:E].bitcast(F32),
                                  ALU.subtract).then_inc(w16_ready, 1)

            for m in range(PAIRS + 3):
                n, o, x, r = m, m - 1, m - 2, m - 3
                if n < PAIRS:
                    for j in range(SB):
                        dve.wait_ge(score_ps, SB * n + j + 1)
                        dve.tensor_reduce(mx[:, 4 * n + j:4 * n + j + 1], score_bank(j), AXX, ALU.max)
                    if n == 0:
                        dve.wait_ge(k_ps, 2)
                        dve.tensor_copy(kT[:, 1, :], k_banks[1][:, :]).then_inc(k_dve, 1)
                if 0 <= r:
                    router_max(r)
                if n < PAIRS:
                    dve.wait_ge(tail_ps, n + 1)
                    if n >= 1:
                        dve.wait_ge(exp_done, 4 * n)
                    link(dve.tensor_tensor(tails[:, :], tail[:, 0:P], mask[:, :], ALU.add))
                    link(dve.tensor_reduce(mx[:, 4 * n + 3:4 * n + 4], tails[:, :], AXX, ALU.max))
                    dve.tensor_reduce(nm[:, n:n + 1], mx[:, 4 * n:4 * n + 4], AXX, ALU.max,
                                      negate=True).then_inc(negmax_ready, 1)
                    if n == 0:
                        dve.wait_ge(v_ps, 2)
                        dve.tensor_copy(vn[:, 2:4, :], v_banks[1][:, :]).then_inc(v_dve, 1)
                if 0 <= x < PAIRS:
                    dve.wait_ge(wo_ps, x + 1)
                    dve.tensor_tensor(x1[:, x, :], x0[:, x, :], mb[:, D:2 * D], ALU.add).then_inc(x1_ready, 1)
                    dve.wait_ge(x1_ready, x + 1)
                    layernorm(x1, x, x + 1, xn2_ready)
                if 0 <= r and m != PAIRS:
                    router_weights(r)
                if 0 <= o < PAIRS:
                    dve.wait_ge(exp_done, 4 * o + 4)
                    link(dve.tensor_reduce(rsum[:, o:o + 1], rs[:, 4 * o:4 * o + 4], AXX, ALU.add))
                    link(dve.reciprocal(rinv[:, o:o + 1], rsum[:, o:o + 1]))
                    dve.wait_ge(pv_ps, o + 1)
                    if o >= 1:
                        dve.wait_ge(oT_ps, o)
                    dve.tensor_scalar(on[:, :], ob[:, 0:D], rinv[:, o:o + 1], None, ALU.mult).then_inc(on_ready, 1)
                if n < PAIRS:
                    dve.wait_ge(pt_ps, 4 * n + 2)
                    if n >= 1:
                        dve.wait_ge(pv_ps, n)
                    dve.tensor_copy(probsT[0:CP, BANK:2 * BANK], pt_banks[1][0:CP, :]).then_inc(pt_dve, 1)
                    dve.wait_ge(pt_ps, 4 * n + 4)
                    dve.tensor_copy(probsT[:, CH * P:(CH + 1) * P], pt_banks[SB][:, 0:P]).then_inc(pt_dve, 1)
                if 0 <= x < PAIRS:
                    dve.wait_ge(x2hi_ready, x + 1)
                    dve.tensor_tensor(x2lo[:, :, x * PT:(x + 1) * PT].rearrange("p k (h s) -> p k h s", h=2),
                                      halves(x2T_cols),
                                      x2hi[:, :, x * PT:(x + 1) * PT].bitcast(F32).rearrange("p k (h s) -> p k h s", h=2),
                                      ALU.subtract).then_inc(x2lo_ready, 1)
                if m == PAIRS:
                    router_weights(r)

            def gated(u):
                dve.wait_ge(silu_done, u + 1)
                dve.wait_ge(up_ready, u + 1)
                dve.tensor_tensor(sw[u % 2], sil[u % 2], up_bank[u], ALU.mult).then_inc(sw_done, 1)

            def weighted(u):
                dve.wait_ge(sw_done, u + 1)
                if u % IC == 0:
                    dve.wait_ge(wb_ready, u // IC + 1)
                for t in token_parts(u):
                    dve.tensor_tensor(hid[u % 2][:, t], sw[u % 2][:, t], wbs[u // IC % 2][:, t],
                                      ALU.mult).then_inc(hid_done, 1)
                for i, t in enumerate(token_parts(u)):
                    dve.wait_ge(hhi_done, u + 1 + i)
                    if u >= 2:
                        dve.wait_ge(down_done, u - 1)
                    dve.tensor_tensor(hlo[u % 2][:, t], hid[u % 2][:, t], hhi[u % 2][:, t].bitcast(F32),
                                      ALU.subtract).then_inc(hlo_done, 1)

            def split_lo(u):
                dve.wait_ge(whi_done, u + 1)
                dve.tensor_tensor(wlo[u // IC % 2][:, chunk_cols(u)], packed(u),
                                  whi[u // IC % 2][:, chunk_cols(u)].bitcast(F32), ALU.subtract).then_inc(wlo_done, 1)

            gated(0)
            gated(1)
            for u in range(2, IC):
                weighted(u - 2)
                gated(u)
            weighted(IC - 2)
            weighted(IC - 1)
            split_lo(2 * IC)
            for u in range(IC, UNITS):
                gated(u)
                weighted(u)
                if u + IC + 1 < UNITS:
                    split_lo(u + IC + 1)

            dve.wait_ge(down_done, UNITS)
            for h in range(2):
                c, t = slice(h * D, (h + 1) * D), slice(h * HT, (h + 1) * HT)
                dve.tensor_copy(halves(xnT[:, 1, c].rearrange("p (n t) -> p n t", n=2)),
                                y_ps[1][:, t].rearrange("p (n h s) -> p n h s", n=2, h=2)).then_inc(yT_dve, 1)
            for n in range(PAIRS):
                src = (scores[:, n * BANK:n * BANK + D] if n < SB else tail[:, 0:D])
                dve.wait_ge(y_ps_ready, n + 1)
                dve.tensor_tensor(fin[:, n, :], x1[:, n, :], src, ALU.add).then_inc(fin_ready, 1)

        @block.tensor
        def _(pe):
            mm = nc.tensor.matmul

            def transpose(dst, src, last=None):
                ins = nc.tensor.transpose(dst, src, ident[0:src.shape[0], 0:src.shape[0]])
                if last is not None:
                    ins.then_inc(last, 1)

            pe.wait_ge(consts_ready, IDENT_STEPS)
            for i in range(WARM):
                mm(tail[:, 0:P], ident[:, :], ident[:, :], start=True, stop=True)

            def project_queries(h):
                pe.wait_ge(xnT_act, h + 1)
                pe.wait_ge(xnT_dve, h + 1)
                c = slice(h * D, (h + 1) * D)
                for m in range(KD):
                    for k in range(KD):
                        ins = mm(q_banks[h][m][:, c], wp[:, 0, k, m * P:(m + 1) * P], xnT[:, k, c], start=k == 0,
                                 stop=k == KD - 1)
                    ins.then_inc(q_ps, 1)

            def project_keys(m):
                pe.wait_ge(*((q_act, 1), (q_dve, 1))[m])
                for k in range(KD):
                    ins = mm(k_banks[m][:, :], wp[:, 1, k, m * P:(m + 1) * P], xnT[:, k, :], start=k == 0,
                             stop=k == KD - 1)
                ins.then_inc(k_ps, 1)

            def project_values(i):
                pe.wait_ge(*((q_act, 2), (q_dve, 2))[i])
                for n in (2 * i, 2 * i + 1):
                    for k in range(KD):
                        ins = mm(v_banks[i][:, (n % 2) * D:(n % 2 + 1) * D], xnT[:, k, n * P:(n + 1) * P],
                                 wp[:, 2, k, :], start=k == 0, stop=k == KD - 1)
                ins.then_inc(v_ps, 1)

            for h in range(2):
                pe.wait_ge(xn_ready, 2 * h + 2)
                for k in range(KD):
                    for n in (2 * h, 2 * h + 1):
                        transpose(xnT_banks[h][k][:, n * P:(n + 1) * P], xn[:, n, k * P:(k + 1) * P], xnT_ps if n % 2 else None)
            pe.wait_ge(wp_in, 16)
            project_queries(0)
            project_queries(1)
            project_keys(0)

            def logits(r):
                pe.wait_ge(x2f_ready, r + 1)
                pe.wait_ge(x2lo_ready, r + 1)
                if r == 0:
                    pe.wait_ge(rw_in, 16)
                for k in range(KD):
                    ins = mm(logit_cols, x2T[:, k, :], rws[:, k, :], start=k == 0, stop=k == KD - 1)
                ins.then_inc(logit_ps, 1)

            def gate_up(u, tokens=slice(0, TOK)):
                pe.wait_ge(whi_done, u + 1)
                lo_split(pe, u)
                (gate_hi, up_hi, _), (gate_lo, up_lo, _) = tiles(whi, u), tiles(wlo, u)
                for dst, hi, lo, ready, freed in ((gate_bank[u], gate_hi, gate_lo, gate_ready, silu_done),
                                                  (up_bank[u], up_hi, up_lo, up_ready, sw_done)):
                    if u > 2:
                        pe.wait_ge(freed, 1 if u == 4 else u - 1)
                    n = 0
                    for k in range(KD):
                        for w, xx in ((hi, x2hi), (hi, x2lo), (lo, x2hi)):
                            ins = mm(dst[:, tokens], w[k], xx[:, k, tokens], start=n == 0, stop=n == 3 * KD - 1)
                            n += 1
                    if tokens.stop == TOK:
                        ins.then_inc(ready, 1)

            def down(u):
                hi, lo = tiles(whi, u)[2], tiles(wlo, u)[2]
                parts = token_parts(u)
                for p, t in enumerate(parts):
                    pe.wait_ge(hhi_done, u + 1 + p)
                    pe.wait_ge(hlo_done, u + 1 + p)
                    for m in range(KD):
                        for i, (w, h) in enumerate(((hi, hhi), (hi, hlo), (lo, hhi))):
                            ins = mm(y_ps[m][:, t], w[m], h[u % 2][:, t], start=u == 0 and i == 0,
                                     stop=u == UNITS - 1 and p == len(parts) - 1 and i == 2)
                ins.then_inc(down_done, 1)

            def weight_rows(e):
                if e >= 1:
                    pe.wait_ge(wb_ready, e)
                mm(wb_ps, sel[:, e, :], w16T[:, :], start=True, stop=True).then_inc(wb_ps_ready, 1)

            def output_projection(x):
                if x == 0:
                    pe.wait_ge(wo_in, 16)
                pe.wait_ge(oT_ready, x + 1)
                for k in range(KD):
                    ins = mm(mb[:, D:2 * D], oT[:, k * P:(k + 1) * P], wp[:, 3, k, :], start=k == 0, stop=k == KD - 1)
                ins.then_inc(wo_ps, 1)

            def weighted_sum(o, j):
                pe.wait_ge(*((pt_dve, 2 * o + 1) if j % 2 else (pt_act, 2 * o + j // 2 + 1)))
                rows_arrived(pe, 2 * o, j)
                rows_arrived(pe, 2 * o + 1, j)
                for c in range(GC * j, GC * (j + 1)):
                    for h in range(2):
                        mm(ob[h * HALF:(h + 1) * HALF, 0:D], probsT[0:CP, c * P + h * HALF:c * P + (h + 1) * HALF],
                           rows[(2 * o + h) % NSLOTS][0:CP, c * D:(c + 1) * D], start=c == 0, stop=False,
                           tile_position=(0, h * HALF), skip_group_check=True)

            for m in range(PAIRS + 3):
                n, o, x, r = m, m - 1, m - 2, m - 3
                if n < PAIRS:
                    if n == 0:
                        pe.wait_ge(q_act, 1)
                        pe.wait_ge(q_dve, 1)
                    for j in range(SB):
                        if j < 2:
                            ring_arrived(pe, 2 * n, j)
                            ring_arrived(pe, 2 * n + 1, j)
                        if n >= 1:
                            pe.wait_ge(*((exp_done, 4 * n - 3), (pt_dve, 2 * n), (pt_act, 2 * n))[j])
                        for k in range(KD):
                            for h in range(2):
                                c = (KD * j + k) * SC
                                ins = mm(scores[h * HALF:(h + 1) * HALF, j * BANK:j * BANK + SC],
                                         qT[:, k, n * P + h * HALF:n * P + (h + 1) * HALF],
                                         ring[(2 * n + h) % TSLOTS][:, c:c + SC],
                                         start=k == 0, stop=k == KD - 1, tile_position=(0, h * HALF))
                        ins.then_inc(score_ps, 1)
                if n == 0:
                    project_keys(1)
                    project_values(0)
                    pe.wait_ge(k_act, 1)
                    pe.wait_ge(k_dve, 1)
                if n < PAIRS:
                    if 0 <= r:
                        logits(r)
                    if 0 <= x:
                        output_projection(x)
                        pe.wait_ge(x2lo_ready, x)
                    if 0 <= r:
                        pe.wait_ge(rexp_done, r + 1)
                    for k in range(KD):
                        ins = mm(tail[:, 0:P], qT[:, k, n * P:(n + 1) * P], kT[:, k, n * P:(n + 1) * P],
                                 start=k == 0, stop=k == KD - 1)
                    ins.then_inc(tail_ps, 1)
                    if n == 0:
                        project_values(1)
                if 0 <= o < PAIRS:
                    if o >= 1:
                        pe.wait_ge(on_ready, o)
                    weighted_sum(o, 0)
                if n >= PAIRS:
                    if r < PAIRS:
                        logits(r)
                    if x < PAIRS:
                        output_projection(x)
                if x == PAIRS - 1:
                    gate_up(0, slice(0, HT))
                    gate_up(1, slice(0, HT))
                if 0 <= o < PAIRS:
                    for j in range(1, SB):
                        weighted_sum(o, j)
                    pe.wait_ge(pt_dve, 2 * o + 2)
                    if o == 0:
                        pe.wait_ge(v_act, 1)
                        pe.wait_ge(v_dve, 1)
                    mm(ob[:, 0:D], probsT[:, CH * P:(CH + 1) * P], vn[:, o, :], start=False, stop=True,
                       skip_group_check=True).then_inc(pv_ps, 1)
                if n < PAIRS:
                    for j in range(SB + 1):
                        pe.wait_ge(exp_done, 4 * n + j + 1)
                        if n >= 1 and j < 2:
                            pe.wait_ge(pt_dve if j else pt_act, 2 * n - 1)
                        if n == 0 and j < 2:
                            pe.wait_ge(v_dve if j else v_act, 1)
                        if j < SB:
                            for i in range(GC):
                                c = GC * j + i
                                transpose(pt_banks[j][0:CP, i * P:(i + 1) * P], probs[:, c * CP:(c + 1) * CP],
                                          pt_ps if i == GC - 1 else None)
                        else:
                            transpose(pt_banks[SB][:, 0:P], probs[:, KV:KV + P], pt_ps)
                if 0 <= x < PAIRS:
                    pe.wait_ge(xn2_ready, x + 1)
                    if x >= 1:
                        pe.wait_ge(rexp_done, x)
                    for k in range(KD):
                        transpose(x2T_cols[:, k, :], xn[:, x, k * P:(k + 1) * P], x2T_ps if k == KD - 1 else None)
                    if x == PAIRS - 1:
                        gate_up(2, slice(0, HT))
                if 0 <= o < PAIRS:
                    pe.wait_ge(on_ready, o + 1)
                    if o >= 1:
                        pe.wait_ge(x1_ready, o)
                    for k in range(KD):
                        transpose(mb[:, k * P:(k + 1) * P], on[:, k * P:(k + 1) * P], oT_ps if k == KD - 1 else None)

            gate_up(0, slice(HT, TOK))
            gate_up(1, slice(HT, TOK))
            pe.wait_ge(w16_ready, PAIRS)
            for n in range(PAIRS):
                transpose(mb[0:2 * E, n * P:(n + 1) * P], w16[:, n, :].bitcast(F32), w16T_ps if n == PAIRS - 1 else None)
            gate_up(2, slice(HT, TOK))
            pe.wait_ge(w16T_ready, 1)
            pe.wait_ge(sel_ready, 1)
            pe.wait_ge(rexp_done, PAIRS)
            weight_rows(0)
            gate_up(3)
            gate_up(4)
            pe.wait_ge(silu_done, 3)
            pe.wait_ge(sw_done, 3)
            down(0)
            down(1)
            weight_rows(1)
            down(2)
            for u in range(5, UNITS):
                gate_up(u)
                down(u - 2)
                if u % IC == 3 and u // IC + 1 < E:
                    weight_rows(u // IC + 1)
            down(UNITS - 2)
            down(UNITS - 1)

            for n in range(PAIRS):
                pe.wait_ge(yT_act, n // 2 + 1)
                pe.wait_ge(yT_dve, n // 2 + 1)
                dst = scores[:, n * BANK:n * BANK + D] if n < SB else tail[:, 0:D]
                for k in range(KD):
                    transpose(dst[:, k * P:(k + 1) * P], xnT[:, k, n * P:(n + 1) * P], y_ps_ready if k == KD - 1 else None)


def kernel(x, ctx_2048, mask_BxSx4224_bf0, L0_xattn_wq, L0_xattn_wk, L0_xattn_wv, L0_xattn_wo,
           L0_ffn_router_w, L0_ffn_gate_w, L0_ffn_up_w, L0_ffn_down_w):
    import concourse.bacc as bacc
    from concourse.bass_utils import run_bass_kernel_spmd

    x = np.asarray(x)
    ctx = np.asarray(ctx_2048)
    xp = np.zeros((2, HALF, PAIRS, D), x.dtype)
    xp[:, :SQ] = x.reshape(PAIRS, 2, SQ, D).transpose(1, 2, 0, 3)
    proj = np.stack([np.asarray(w).T.reshape(KD, P, D).transpose(1, 0, 2)
                     for w in (L0_xattn_wq, L0_xattn_wk, L0_xattn_wv, L0_xattn_wo)], axis=1)
    router = np.asarray(L0_ffn_router_w).T.reshape(KD, P, E).transpose(1, 0, 2)
    ctx_t = ctx.reshape(B, CP, SB, GC, KD, P).transpose(0, 5, 2, 4, 3, 1).reshape(B, P, KD * KV)
    ctx_n = np.zeros((B, P, CH * D), ctx.dtype)
    ctx_n[:, :CP] = ctx.reshape(B, CP, CH * D)

    def by_chunk(w):
        return np.asarray(w).reshape(E, IC, P, KD, P).transpose(0, 4, 1, 3, 2).reshape(E, P, IC, KD * P)

    down = np.asarray(L0_ffn_down_w).reshape(E, D, IC, P).transpose(0, 3, 2, 1)
    wffn = np.concatenate([by_chunk(L0_ffn_gate_w), by_chunk(L0_ffn_up_w), down], axis=3).reshape(E, P, WCOLS)

    arrays = {"xp": xp.reshape(P, PAIRS, D), "wproj": proj, "router": router,
              "ctx_t": ctx_t, "ctx_n": ctx_n, "wffn": wffn}
    arrays = {k: np.ascontiguousarray(v) for k, v in arrays.items()}
    nc = bacc.Bacc("TRN2", target_bir_lowering=False, num_devices=1)
    args = [nc.dram_tensor(k, v.shape, mybir.dt.from_np(v.dtype), kind="ExternalInput").ap() for k, v in arrays.items()]
    args.append(nc.dram_tensor("out", (B, SQ, D), F32, kind="ExternalOutput").ap())
    build(nc, *args)
    result = run_bass_kernel_spmd(nc, [arrays], core_ids=[0])
    return result.results[0]["out"]
```
